# Optimizing a Trainium2 kernel written in Bass

```python
import numpy as np
import jax
import jax.numpy as jnp

def _softmax(x, axis=-1):
    return jax.nn.softmax(x, axis=axis)

def _gelu(x):
    return jax.nn.gelu(x, approximate=True)

def _silu(x):
    return jax.nn.silu(x)

def _sigmoid(x):
    return jax.nn.sigmoid(x)

def _layernorm(x, axis=-1, eps=1e-05):
    m = jnp.mean(x, axis=axis, keepdims=True)
    v = jnp.var(x, axis=axis, keepdims=True)
    return (x - m) / jnp.sqrt(v + eps)

def _scatter_add(tgt, idx, src, axis=0):
    return tgt.at[idx].add(src)

def _segment_sum(src, seg, n):
    return jax.ops.segment_sum(src, seg, n)
kernel_name = 'mk_adaln_ffn_d2_seqx_r8_ce6529'

def setup_inputs(seed: int=0):
    np.random.seed(seed)
    _w = jnp.asarray

    def _rec_inputs():
        import jax
        import jax.numpy as jnp
        _rk = jax.random.key(seed)
        x = -7.109e-05 + 0.9999 * jax.random.normal(jax.random.fold_in(_rk, 1), (8, 128, 512), jnp.float32)
        _lenS = 128 - jax.random.randint(jax.random.fold_in(_rk, 7), (8,), 0, max(1, 128 // 4) + 1, jnp.int32)
        _lenS2 = 128 - jax.random.randint(jax.random.fold_in(_rk, 8), (8,), 0, max(1, 128 // 4) + 1, jnp.int32)
        itok_B_9_3973 = jax.random.randint(jax.random.fold_in(_rk, 11), (8,), 9, 3974, jnp.int32)
        condB_codebook = -0.0625 + 0.715345 * jax.random.normal(jax.random.fold_in(_rk, 12), (8,), jnp.float32)
        return (x, itok_B_9_3973, condB_codebook)
    x, itok_B_9_3973, condB_codebook = _rec_inputs()

    def _L0_cond_setup():
        import jax, jax.numpy as jnp
        import numpy as np
        from jax import lax
        B, E, T = (32, 64, 512)
        K = 5
        PAD = (K - 1) // 2
        key = jax.random.key(seed)
        k1, k2, k3 = jax.random.split(key, 3)
        x = jax.random.normal(k1, (B, E, T), dtype=jnp.float32)
        length = jax.random.randint(k2, (B,), 1, T + 1, dtype=jnp.int64)
        conv_w = jax.random.normal(k3, (1, 1, K), dtype=jnp.float32) * (1.0 / np.sqrt(K))
        return {'x': x, 'length': length, 'conv_w': conv_w}
    _L0_cond_all = _L0_cond_setup()
    _L0_cond_in = {k: v for k, v in _L0_cond_all.items() if k in ('conv_w',)}
    del _L0_cond_all

    def _L0_ffn_setup():
        import jax, jax.numpy as jnp
        import numpy as np
        EPS = 1e-05

        def _act_quant(x):
            scale = 127.0 / jnp.clip(jnp.max(jnp.abs(x), axis=-1, keepdims=True), EPS)
            xq = jnp.clip(jnp.round(x * scale), -128.0, 127.0) / scale
            return x + jax.lax.stop_gradient(xq - x)

        def _weight_quant(w):
            scale = jnp.clip(jnp.mean(jnp.abs(w)), EPS)
            wq = jnp.clip(jnp.round(w / scale), -1.0, 1.0) * scale
            return w + jax.lax.stop_gradient(wq - w)

        def _bitlinear(x, w):
            return jnp.einsum('bsh,oh->bso', _act_quant(x), _weight_quant(w))
        key = jax.random.key(seed)
        k1, k2, k3, k4 = jax.random.split(key, 4)
        B, S, H, I = (4, 256, 512, 1376)
        x = jax.random.normal(k1, (B, S, H), dtype=jnp.float32)
        w_gate = jax.random.normal(k2, (I, H), dtype=jnp.float32) * (1.0 / np.sqrt(H))
        w_up = jax.random.normal(k3, (I, H), dtype=jnp.float32) * (1.0 / np.sqrt(H))
        w_down = jax.random.normal(k4, (H, I), dtype=jnp.float32) * (1.0 / np.sqrt(I))
        return {'x': x, 'w_gate': w_gate, 'w_up': w_up, 'w_down': w_down}
    _L0_ffn_all = _L0_ffn_setup()
    _L0_ffn_in = {k: v for k, v in _L0_ffn_all.items() if k in ('w_gate', 'w_up', 'w_down')}
    del _L0_ffn_all

    def _L1_cond_setup():
        import jax, jax.numpy as jnp
        import numpy as np
        GROUP = 128
        LORA_ALPHA = 32.0
        LORA_RANK = 64
        key = jax.random.key(seed)
        k1, k2, k3, k4 = jax.random.split(key, 4)
        O, I = (512, 512)
        x = jax.random.normal(k1, (4, 256, I), dtype=jnp.float32)
        weight = jax.random.normal(k2, (O, I), dtype=jnp.float32) * 0.02
        wg = weight.reshape(O, I // GROUP, GROUP)
        scale_log = jnp.log(jnp.clip(jnp.max(jnp.abs(wg), axis=2, keepdims=True), 1e-05))
        codebook = jnp.array([-1.0, -0.25, 0.0, 1.0], dtype=jnp.float32)
        lora_A = jax.random.normal(k3, (LORA_RANK, I), dtype=jnp.float32) * 0.02
        lora_B = jax.random.normal(k4, (O, LORA_RANK), dtype=jnp.float32) * 0.02
        return {'x': x, 'weight': weight, 'scale_log': scale_log, 'codebook': codebook, 'lora_A': lora_A, 'lora_B': lora_B}
    _L1_cond_all = _L1_cond_setup()
    _L1_cond_in = {k: v for k, v in _L1_cond_all.items() if k in ('weight', 'scale_log', 'lora_A', 'lora_B')}
    del _L1_cond_all

    def _L1_ffn_setup():
        import jax, jax.numpy as jnp
        import numpy as np
        SCALING = 16.0 / 8.0
        GAMMA = 1.0
        EPS = 1e-12
        key = jax.random.key(seed)
        ks = jax.random.split(key, 8)
        B, T, H, O = (4, 256, 512, 512)
        E_tot, E_act, r = (16, 4, 8)
        return {'x': jax.random.normal(ks[0], (B, T, H), jnp.float32), 'W_base': jax.random.normal(ks[1], (O, H), jnp.float32) * 0.02, 'b_base': jax.random.normal(ks[2], (O,), jnp.float32) * 0.02, 'lora_A': jax.random.normal(ks[3], (E_tot, r, H), jnp.float32) * 0.02, 'lora_B': jax.random.normal(ks[4], (E_tot, O, r), jnp.float32) * 0.02, 'router_W': jax.random.normal(ks[5], (E_tot, H), jnp.float32) * 0.02, 'router_b': jax.random.normal(ks[6], (E_tot,), jnp.float32) * 0.02, 'domain_prior': jax.random.uniform(ks[7], (E_tot,), jnp.float32), 'active': jnp.arange(E_act, dtype=jnp.int32)}
    _L1_ffn_all = _L1_ffn_setup()
    _L1_ffn_in = {k: v for k, v in _L1_ffn_all.items() if k in ('W_base', 'b_base', 'lora_A', 'lora_B', 'router_W', 'router_b', 'domain_prior', 'active')}
    del _L1_ffn_all
    return {'x': x, 'itok_B_9_3973': itok_B_9_3973, 'condB_codebook': condB_codebook, 'L0_cond_conv_w': _L0_cond_in['conv_w'], 'L0_ffn_w_gate': _L0_ffn_in['w_gate'], 'L0_ffn_w_up': _L0_ffn_in['w_up'], 'L0_ffn_w_down': _L0_ffn_in['w_down'], 'L1_cond_weight': _L1_cond_in['weight'], 'L1_cond_scale_log': _L1_cond_in['scale_log'], 'L1_cond_lora_A': _L1_cond_in['lora_A'], 'L1_cond_lora_B': _L1_cond_in['lora_B'], 'L1_ffn_W_base': _L1_ffn_in['W_base'], 'L1_ffn_b_base': _L1_ffn_in['b_base'], 'L1_ffn_lora_A': _L1_ffn_in['lora_A'], 'L1_ffn_lora_B': _L1_ffn_in['lora_B'], 'L1_ffn_router_W': _L1_ffn_in['router_W'], 'L1_ffn_router_b': _L1_ffn_in['router_b'], 'L1_ffn_domain_prior': _L1_ffn_in['domain_prior'], 'L1_ffn_active': _L1_ffn_in['active']}

def reference(x, itok_B_9_3973, condB_codebook, L0_cond_conv_w, L0_ffn_w_gate, L0_ffn_w_up, L0_ffn_w_down, L1_cond_weight, L1_cond_scale_log, L1_cond_lora_A, L1_cond_lora_B, L1_ffn_W_base, L1_ffn_b_base, L1_ffn_lora_A, L1_ffn_lora_B, L1_ffn_router_W, L1_ffn_router_b, L1_ffn_domain_prior, L1_ffn_active):
    import jax
    import jax.numpy as jnp

    def _L0_cond_ref(x, length, conv_w):
        import jax, jax.numpy as jnp
        import numpy as np
        from jax import lax
        B, E, T = (32, 64, 512)
        K = 5
        PAD = (K - 1) // 2
        mask = (jnp.arange(T)[None, :] < length[:, None]).astype(x.dtype)
        denom = length.astype(x.dtype)[:, None]
        y = jnp.einsum('bet,bt->be', x, mask) / denom
        yc = lax.conv_general_dilated(y[:, None, :], conv_w, window_strides=(1,), padding=[(PAD, PAD)], dimension_numbers=('NCH', 'OIH', 'NCH'))[:, 0, :]
        gate = jax.nn.sigmoid(yc)
        return x * gate[:, :, None]

    def _L0_ffn_ref(x, w_gate, w_up, w_down):
        import jax, jax.numpy as jnp
        import numpy as np
        EPS = 1e-05

        def _act_quant(x):
            scale = 127.0 / jnp.clip(jnp.max(jnp.abs(x), axis=-1, keepdims=True), EPS)
            xq = jnp.clip(jnp.round(x * scale), -128.0, 127.0) / scale
            return x + jax.lax.stop_gradient(xq - x)

        def _weight_quant(w):
            scale = jnp.clip(jnp.mean(jnp.abs(w)), EPS)
            wq = jnp.clip(jnp.round(w / scale), -1.0, 1.0) * scale
            return w + jax.lax.stop_gradient(wq - w)

        def _bitlinear(x, w):
            return jnp.einsum('bsh,oh->bso', _act_quant(x), _weight_quant(w))
        gate = jax.nn.silu(_bitlinear(x, w_gate))
        up = _bitlinear(x, w_up)
        return _bitlinear(gate * up, w_down)

    def _L1_cond_ref(x, weight, scale_log, codebook, lora_A, lora_B):
        import jax, jax.numpy as jnp
        import numpy as np
        GROUP = 128
        LORA_ALPHA = 32.0
        LORA_RANK = 64
        O, I = weight.shape
        lora_delta = lora_B @ lora_A * (LORA_ALPHA / LORA_RANK)
        cb = codebook / jnp.clip(jnp.max(jnp.abs(codebook)), 1e-08)
        scale = jnp.exp(scale_log)
        wg = (weight + lora_delta).reshape(O, I // GROUP, GROUP)
        normalized = wg / scale
        thresholds = (cb[:-1] + cb[1:]) * 0.5
        idx = jnp.searchsorted(thresholds, normalized, side='left')
        quantized = cb[idx]
        w = jax.lax.stop_gradient(quantized - normalized) + normalized
        w_q = (w * scale).reshape(O, I)
        w_eff = w_q + lora_delta
        return x @ w_eff.T

    def _L1_ffn_ref(x, W_base, b_base, lora_A, lora_B, router_W, router_b, domain_prior, active):
        import jax, jax.numpy as jnp
        import numpy as np
        SCALING = 16.0 / 8.0
        GAMMA = 1.0
        EPS = 1e-12
        y = jnp.einsum('bth,oh->bto', x, W_base) + b_base
        A = lora_A[active]
        Bm = lora_B[active]
        z = jnp.einsum('bth,erh->bter', x, A)
        contribs = jnp.einsum('bter,eor->bteo', z, Bm) * SCALING
        logits = jnp.einsum('bth,eh->bte', x, router_W) + router_b
        logits = logits[..., active]
        prior = domain_prior[active]
        alpha = jax.nn.softmax(jnp.log(prior + EPS) + logits / GAMMA, axis=-1)
        return y + jnp.einsum('bteo,bte->bto', contribs, alpha)
    x = x + _L0_ffn_ref(_L0_cond_ref(x, itok_B_9_3973, L0_cond_conv_w), L0_ffn_w_gate, L0_ffn_w_up, L0_ffn_w_down)
    x = x + _L1_ffn_ref(_L1_cond_ref(x, L1_cond_weight, L1_cond_scale_log, condB_codebook, L1_cond_lora_A, L1_cond_lora_B), L1_ffn_W_base, L1_ffn_b_base, L1_ffn_lora_A, L1_ffn_lora_B, L1_ffn_router_W, L1_ffn_router_b, L1_ffn_domain_prior, L1_ffn_active)
    return x

_drawn_inputs = setup_inputs


def setup_inputs(seed=0):
    import zlib

    import numpy as np

    out = dict(_drawn_inputs(seed))
    spreads = {}
    factors = {'L0_cond_conv_w': 32.942,
     'L1_ffn_b_base': 2.863,
     'L1_ffn_lora_A': 7.843,
     'L1_ffn_lora_B': 7.832,
     'L1_ffn_router_W': 8.0,
     'L1_ffn_router_b': 8.0,
     'L1_ffn_domain_prior': 8.0}
    for name, (base, spread) in spreads.items():
        noise = np.random.default_rng([zlib.crc32(name.encode()), seed]).standard_normal(out[name].shape)
        drawn = base * np.exp(spread * noise) if base else spread * noise
        out[name] = jnp.asarray(drawn.astype(out[name].dtype))
    for name, factor in factors.items():
        out[name] = (out[name] * factor).astype(out[name].dtype)
    return out
```

```python
from contextlib import ExitStack

import concourse.bass as bass
from concourse import mybir

F32 = mybir.dt.float32
F32R = mybir.dt.float32r
BF16 = mybir.dt.bfloat16
I16 = mybir.dt.int16
I32 = mybir.dt.int32
ALU = mybir.AluOpType
ACT = mybir.ActivationFunctionType
AX = mybir.AxisListType

P = 128
NB, E, H = 8, 128, 512
F = 1376
KH = H // P
KF = -(-F // P)
FL = F - (KF - 1) * P
CHUNKS = [(0, 464), (464, 464), (928, 448)]
NC = len(CHUNKS)
NCB = 8
NT = NCB - 1
GROUP = 128
RANK0 = 64
NE, NACT, RK = 16, 4, 8
ZC = NACT * RK
ZL = ZC + NACT
MC = H + ZL
ZS = 3 * ZC + 2
TAPS = 5
NW = float(F * H)
QMAX = 127.0
EPS = 1e-5
DOWN_PARTS = [(0, 3, P), (3, 3, P), (6, 2, P), (8, 2, P), (KF - 1, 1, FL)]


def build(nc, x, length, codebook, conv_w, w_gate_t, w_up_t, w_down_t, cond_w, scale_log,
          lora0_a, lora0_b_t, w_base_t, b_base, lora1_a, lora1_b_t, router_w, router_b, prior,
          active, out):
    with ExitStack() as ctx:
        def sb(name, shape, dt=F32):
            return ctx.enter_context(nc.sbuf_tensor(name, shape, dt))

        def sem(name):
            return ctx.enter_context(nc.semaphore(name))

        bank = [ctx.enter_context(nc.psum_tensor(f"bank{i}", [P, 512], F32)) for i in range(8)]
        bank_hT = [bank[0][:].bitcast(BF16), bank[1][:].bitcast(BF16)]
        bank_down = bank[2]
        bank_xT = bank[3][:].bitcast(BF16)
        bank_zl = bank[3]
        bank_g = [bank[4], bank[6]]
        bank_u = [bank[5], bank[7]]

        xs = sb("xs", [P, NB, H])
        raw = [sb("raw_gate_down", [P, KF * H]), sb("raw_up", [P, KH * F])]
        raw_gate = raw[0][:, 0:KH * F].rearrange("p (k f) -> p k f", k=KH)
        raw_up = raw[1][:, :].rearrange("p (k f) -> p k f", k=KH)
        raw_down = raw[0][:, :].rearrange("p (j h) -> p j h", j=KF)
        cond = sb("cond", [P, KH, H])
        wcat = sb("wcat", [P, KH, MC])
        lora = [sb("lora_a_xq_i", [P, H]), sb("lora_bt_xq_b", [P, H])]
        lora_a, lora_bt = lora[0][0:RANK0, :], lora[1][0:RANK0, :]
        slog = sb("slog", [P, KH, KH])
        cb = sb("cb", [P, NCB])
        cw = sb("cw", [P, TAPS])
        len_i = sb("len_i", [P, NB], I32)
        act_i = sb("act_i", [P, NACT], I32)
        l1a = sb("l1a", [NE * RK, H])
        l1b = sb("l1b", [NE * RK, H])
        rw = sb("rw", [NE, H])
        pr = sb("pr", [NE, 2])
        bb = sb("bb", [1, H])

        t_iota = sb("t_iota", [P, H])
        diff = sb("diff", [P, P])
        pick = sb("pick", [P, NACT, RK])
        part = sb("part", [P, 1])
        ident = sb("ident", [P, P])
        ident_b = sb("ident_b", [P, P], BF16)
        ones = sb("ones", [P, P])
        bias_rows = sb("bias_rows", [1, ZS])
        low_row = sb("low_row", [P, 1])
        sign_row = sb("sign_row", [P, 1])
        tmp_row = sb("tmp_row", [P, 1])

        cbm = sb("cbm", [P, 4])
        cbn = sb("cbn", [P, NCB])
        th = sb("th", [P, NT])
        step = sb("step", [P, NT])
        step_h = sb("step_h", [P, NT], F32R)
        step_l = sb("step_l", [P, NT])
        diag_h = sb("diag_h", [P, NB, P], F32R)
        diag_l = sb("diag_l", [P, NT, P], F32R)
        scl = sb("scl", [P, KH, KH])
        scl_inv = sb("scl_inv", [P, KH, KH])
        delta = sb("delta", [P, KH, H])
        fr = sb("fr", [P, 4, KH * H], F32R)
        mask = [fr[:, i, :].rearrange("p (k h) -> p k h", k=KH) for i in range(4)]
        x1t_h = fr[:, 0:2, :].rearrange("p a (b k e) -> p (a b) k e", b=4, k=KH)
        x1t_l = fr[:, 2:4, :].rearrange("p a (b k e) -> p (a b) k e", b=4, k=KH)

        junk = sb("junk", [P, H])
        act_f = sb("act_f", [P, NACT])
        act_n = sb("act_n", [P, NACT])
        act8 = sb("act8", [P, NACT])
        sel_er = sb("sel_er", [P, ZS])
        sel_e = sb("sel_e", [NE, NACT])
        pr_bc = sb("pr_bc", [NE, 2, P])
        log_prior = sb("log_prior", [P, NACT])
        eps12 = sb("eps12", [P, 1])
        b_full = junk[0:ZS, :]
        b_high = sb("b_high", [ZS, H], F32R)
        b_stack = sb("b_stack", [ZS, H], F32R)

        len_f = sb("len_f", [P, NB])
        len_r = sb("len_r", [P, NB])
        ysum = sb("ysum", [P, NB])
        ymean = sb("ymean", [P, NB])
        band = sb("band", [P, P])
        band_t = sb("band_t", [P, P])
        yexp = sb("yexp", [P, NB])
        gate = sb("gate", [P, NB])
        rmax = sb("rmax", [P, NB])
        arow = sb("arow", [P, NB])
        qx = sb("qx", [P, NB])
        s_g = sb("s_g", [P, NB])
        s_u = sb("s_u", [P, NB])
        wsum = sb("wsum", [P, 3, len(DOWN_PARTS)])
        wtot = sb("wtot", [P, 3])
        wscale = sb("wscale", [P, 3])
        winv = sb("winv", [P, 3])
        w127 = sb("w127", [P, 3])
        tern_g = sb("tern_g", [P, KH, F], BF16)
        tern_u = sb("tern_u", [P, KH, F], BF16)
        tern_d = sb("tern_d", [P, KF, H], BF16)
        junk_a = tern_d[:].rearrange("p j h -> p (j h)")[:, 0:4 * H]
        tern_i = sb("tern_i", [P, 2, KH * CHUNKS[0][1]], I16)
        xq_i = lora[0][:].bitcast(I16).rearrange("p (i h) -> p i h", i=2)
        xq_b = lora[1][:].bitcast(BF16).rearrange("p (i h) -> p i h", i=2)
        xq_t = l1a[:].bitcast(BF16).rearrange("p (i k e) -> p i k e", i=2, k=KH)
        cond_flat = cond[:].rearrange("p k h -> p (k h)")
        silu = cond_flat[:, 0:2 * CHUNKS[0][1]].rearrange("p (i f) -> p i f", i=2)
        res = cond_flat[:, 2 * H:4 * H].rearrange("p (i h) -> p i h", i=2)
        hbuf = [raw[1][:, i * F:(i + 1) * F] for i in range(2)]
        h_i = raw[1][:, 2 * F:3 * F].bitcast(I16).rearrange("p (i f) -> p i f", i=2)
        h_b = raw[1][:, 3 * F:4 * F].bitcast(BF16).rearrange("p (i f) -> p i f", i=2)
        hmax = sb("hmax", [P, 2, NC])
        hred = sb("hred", [P, NB])
        harow = sb("harow", [P, NB])
        hrec = sb("hrec", [P, NB])
        hq = sb("hq", [P, NB])
        s_d = sb("s_d", [P, NB])
        h_t = delta[:].rearrange("p k h -> p (k h)")[:, 0:KF * P].bitcast(BF16)\
            .rearrange("p (i j e) -> p i j e", i=2, j=KF)

        m_h = sb("m_h", [P, KH, MC], F32R)
        m_l = sb("m_l", [P, KH, MC], F32R)
        wcat_flat = wcat[:].rearrange("p k c -> p (k c)")
        zstack = wcat_flat[:, 0:NB * ZS].rearrange("p (b c) -> p b c", b=NB)
        zl = wcat_flat[:, NB * ZS:NB * (ZS + ZL)].rearrange("p (b c) -> p b c", b=NB)
        zz = wcat_flat[:, NB * (ZS + ZL):NB * (ZS + ZL + ZC)].rearrange("p (b c) -> p b c", b=NB)
        lg = sb("lg", [P, NB, NACT])
        lmax = sb("lmax", [P, NB])
        ex = sb("ex", [P, NB, NACT])
        esum = sb("esum", [P, NB])
        alpha = sb("alpha", [P, NB, NACT])
        zz_h = diag_l[:].rearrange("p t c -> p (t c)")[:, 0:NB * ZC].rearrange("p (b c) -> p b c", b=NB)
        zt = diag_h[0:ZS, :, :]

        ld_cond, ld_lora, ld_slog, ld_cb = sem("ld_cond"), sem("ld_lora"), sem("ld_slog"), sem("ld_cb")
        ld_act, ld_conv, ld_exp, ld_wbase = sem("ld_act"), sem("ld_conv"), sem("ld_exp"), sem("ld_wbase")
        ld_x = [sem(f"ld_x{b}") for b in range(NB)]
        ld_gate = [sem(f"ld_gate{k}") for k in range(KH)]
        ld_up = [sem(f"ld_up{k}") for k in range(KH)]
        ld_down = [sem(f"ld_down{i}") for i in range(len(DOWN_PARTS))]
        stored = [sem("stored_even"), sem("stored_odd")]
        iota_done = sem("iota_done")
        ident_done = sem("ident_done")
        eps_done = sem("eps_done")
        delta_ps = sem("delta_ps")
        delta_done = sem("delta_done")
        scl_done = sem("scl_done")
        diag_done = sem("diag_done")
        sel_done = sem("sel_done")
        sel_ps = sem("sel_ps")
        sel_read = sem("sel_read")
        b_ps = sem("b_ps")
        b_done = sem("b_done")
        lp_done = sem("lp_done")
        mask_done = sem("mask_done")
        mask_used = sem("mask_used")
        weff_done = sem("weff_done")
        band_done = sem("band_done")
        conv_ps = sem("conv_ps")
        yexp_done = sem("yexp_done")
        wsum_done = [sem("gsum_done"), sem("usum_done"), sem("dsum_done")]
        wtot_ps = sem("wtot_ps")
        wtot_read = sem("wtot_read")
        winv_done = sem("winv_done")
        tern_int = sem("tern_int")
        tern_out = sem("tern_out")
        fold_ps = sem("fold_ps")
        folds_ps = sem("folds_ps")
        mh_done = sem("mh_done")
        ml_done = sem("ml_done")
        xq_done = sem("xq_done")
        xt_ps = sem("xt_ps")
        xt_done = sem("xt_done")
        gu_ps = sem("gu_ps")
        silu_done = sem("silu_done")
        hmul_done = sem("hmul_done")
        hscale_done = sem("hscale_done")
        hint_done = sem("hint_done")
        hb_done = sem("hb_done")
        ht_ps = sem("ht_ps")
        ht_done = sem("ht_done")
        down_ps = sem("down_ps")
        x1_done = sem("x1_done")
        x1t_ps = sem("x1t_ps")
        x1h_done = sem("x1h_done")
        x1l_done = sem("x1l_done")
        zl_ps = sem("zl_ps")
        zl_done = sem("zl_done")
        lmax_done = sem("lmax_done")
        ex_done = sem("ex_done")
        zs_done = sem("zs_done")
        zt_ps = sem("zt_ps")
        zt_done = sem("zt_done")
        y_ps = sem("y_ps")
        res_done = sem("res_done")
        dve_chain = sem("dve_chain")

        def chunk_no(b, c):
            return NC * b + c

        block = ctx.enter_context(nc.Block())

        @block.sync
        def _(sp):
            cond_v = cond_w.rearrange("(k p) h -> p k h", p=P)
            sp.dma_start(cond[:], cond_v).then_inc(ld_cond, 16)
            for b in range(2):
                sp.dma_start(xs[:, b, :], x[b]).then_inc(ld_x[b], 16)
            gate_v = w_gate_t.rearrange("(k p) f -> p k f", p=P)
            up_v = w_up_t.rearrange("(k p) f -> p k f", p=P)
            for k in range(KH):
                sp.dma_start(raw_gate[:, k, :], gate_v[:, k, :]).then_inc(ld_gate[k], 16)
            for b in range(2, NB):
                sp.dma_start(xs[:, b, :], x[b]).then_inc(ld_x[b], 16)
            sp.dma_start(wcat[:, :, 0:H], w_base_t.rearrange("(k p) c -> p k c", p=P)).then_inc(ld_wbase, 16)
            for k in range(KH):
                sp.dma_start(raw_up[:, k, :], up_v[:, k, :]).then_inc(ld_up[k], 16)
            sp.wait_ge(tern_out, NC)
            for i, (j0, n, rows) in enumerate(DOWN_PARTS):
                src = w_down_t[j0 * P:j0 * P + (n - 1) * P + rows, :].rearrange("(j p) h -> p j h", p=rows)
                sp.dma_start(raw_down[0:rows, j0:j0 + n, :], src).then_inc(ld_down[i], 16)
            for b in range(NB):
                sp.wait_ge(res_done, b + 1)
                sp.dma_start(out[b], res[:, b % 2, :]).then_inc(stored[b % 2], 16)
            for i in range(2):
                sp.wait_ge(stored[i], 16 * (NB // 2))

        @block.gpsimd
        def _(pool):
            pool.iota(diff[:], [[-1, P]], 0, 1, allow_small_or_imprecise_dtypes=True).then_inc(iota_done, 1)
            pool.iota(pick[:], [[0, NACT], [-1, RK]], 0, 1, allow_small_or_imprecise_dtypes=True).then_inc(iota_done, 1)
            pool.iota(part[:], [[0, 1]], 0, 1, allow_small_or_imprecise_dtypes=True).then_inc(iota_done, 1)
            pool.memset(sel_er[:], 0.0).then_inc(iota_done, 1)
            pool.iota(t_iota[:], [[1, H]], 0, 0, allow_small_or_imprecise_dtypes=True).then_inc(iota_done, 1)
            pool.memset(ones[:], 1.0).then_inc(iota_done, 1)
            pool.memset(bias_rows[:, 0:3 * ZC], 0.0).then_inc(iota_done, 1)
            pool.memset(bias_rows[:, 3 * ZC:ZS], 1.0).then_inc(iota_done, 1)

        @block.scalar
        def _(act):
            act.dma_start(lora_bt, lora0_b_t).then_inc(ld_lora, 16)
            act.dma_start(lora_a, lora0_a).then_inc(ld_lora, 16)
            act.dma_start(cb[:], codebook.partition_broadcast(P)).then_inc(ld_cb, 16)
            act.dma_start(slog[:], scale_log.rearrange("(k p) g one -> p k (g one)", p=P)).then_inc(ld_slog, 16)
            act.dma_start(act_i[:], active.partition_broadcast(P)).then_inc(ld_act, 16)
            act.dma_start(cw[:], conv_w.partition_broadcast(P)).then_inc(ld_conv, 16)
            act.dma_start(len_i[:], length.partition_broadcast(P)).then_inc(ld_conv, 16)
            act.dma_start(l1a[:], lora1_a).then_inc(ld_exp, 16)
            act.dma_start(l1b[:], lora1_b_t).then_inc(ld_exp, 16)
            act.dma_start(rw[:], router_w).then_inc(ld_exp, 16)
            act.dma_start(pr[:, 0:1], prior).then_inc(ld_exp, 16)
            act.dma_start(pr[:, 1:2], router_b).then_inc(ld_exp, 16)
            act.dma_start(bb[:], b_base).then_inc(ld_exp, 16)

            act.wait_ge(ld_slog, 16)
            act.activation(scl[:], slog[:], ACT.Exp).then_inc(scl_done, 1)
            for k in range(KH):
                act.wait_ge(delta_ps, k + 1)
                act.activation(delta[:, k, :], bank[4 + k % 2][:], ACT.Copy, scale=0.5).then_inc(delta_done, 1)

            def weight_sum(i, k, src, rows=P):
                n = src.shape[1] * (src.shape[2] if len(src.shape) > 2 else 1)
                dst = junk_a[0:rows, 0:n]
                if k > 0:
                    act.wait_ge(wsum_done[i], k)
                elif i > 0:
                    act.wait_ge(wsum_done[i - 1], KH)
                if len(src.shape) > 2:
                    dst = dst.rearrange("p (j h) -> p j h", j=src.shape[1])
                act.activation(dst, src, ACT.Abs, accum_out=wsum[0:rows, i, k:k + 1]).then_inc(wsum_done[i], 1)

            act.wait_ge(eps_done, 1)
            for k in range(KH):
                act.wait_ge(ld_gate[k], 16)
                weight_sum(0, k, raw_gate[:, k, :])
            act.wait_ge(conv_ps, 1)
            act.activation(yexp[:], bank[4][:, 0:NB], ACT.Exp, scale=-1.0).then_inc(yexp_done, 1)
            act.wait_ge(sel_read, 2)
            act.activation(log_prior[:], lg[:, 0, :], ACT.Ln, bias=eps12[:, 0:1]).then_inc(lp_done, 1)
            for k in range(KH):
                act.wait_ge(ld_up[k], 16)
                weight_sum(1, k, raw_up[:, k, :])
            for k in range(KH):
                act.wait_ge(fold_ps, k + 1)
                act.activation(m_h[:, k, 0:H], bank[k][:], ACT.Copy).then_inc(mh_done, 1)
            act.wait_ge(folds_ps, 1)
            act.activation(m_h[:, :, H:MC], bank[6][:, 0:KH * ZL].rearrange("p (k c) -> p k c", k=KH),
                           ACT.Copy).then_inc(mh_done, 1)

            def silu_chunk(b, c):
                n = chunk_no(b, c)
                w = CHUNKS[c][1]
                act.wait_ge(gu_ps, n + 1)
                if n >= 2:
                    act.wait_ge(hmul_done, n - 1)
                act.activation(silu[:, n % 2, 0:w], bank_g[n % 2][:, 0:w], ACT.Silu,
                               scale=s_g[:, b:b + 1]).then_inc(silu_done, 1)

            def hidden_round(b):
                act.wait_ge(hscale_done, b + 1)
                if b >= 2:
                    act.wait_ge(hb_done, b - 1)
                act.activation(h_i[:, b % 2, :], hbuf[b % 2], ACT.Copy,
                               scale=hq[:, b:b + 1]).then_inc(hint_done, 1)

            def hidden_evacuate(b):
                for half, (j0, j1) in enumerate(((0, 6), (6, KF - 1))):
                    act.wait_ge(ht_ps, 2 * b + half + 1)
                    if b >= 2 and half == 0:
                        act.wait_ge(down_ps, b - 1)
                    src = bank_hT[half]
                    if half == 1:
                        act.activation(h_t[0:FL, b % 2, KF - 1, :], src[0:FL, (j1 - j0) * P:(j1 - j0 + 1) * P],
                                       ACT.Copy).then_inc(ht_done, 1)
                    act.activation(h_t[:, b % 2, j0:j1, :],
                                   src[:, 0:(j1 - j0) * P].rearrange("p (j e) -> p j e", e=P),
                                   ACT.Copy).then_inc(ht_done, 1)

            def x1_high(b):
                act.wait_ge(x1t_ps, b + 1)
                act.activation(x1t_h[:, b, :, :], bank_down[:].rearrange("p (k e) -> p k e", k=KH),
                               ACT.Copy).then_inc(x1h_done, 1)

            for b in range(NB + 2):
                if b < NB:
                    silu_chunk(b, 0)
                if b >= 2:
                    x1_high(b - 2)
                if b == 0:
                    for i, (j0, n, rows) in enumerate(DOWN_PARTS):
                        act.wait_ge(ld_down[i], 16)
                        weight_sum(2, i, raw_down[0:rows, j0:j0 + n, :], rows)
                if b < NB:
                    silu_chunk(b, 1)
                if 1 <= b <= NB:
                    hidden_evacuate(b - 1)
                if b < NB:
                    silu_chunk(b, 2)
                    hidden_round(b)
            act.wait_ge(lmax_done, 1)
            act.activation(ex[:], lg[:], ACT.Exp).then_inc(ex_done, 1)
            for i in range(2):
                act.wait_ge(zt_ps, i + 1)
                act.activation(zt[:, 4 * i:4 * i + 4, :], bank[i][0:ZS, :].rearrange("p (b e) -> p b e", b=4),
                               ACT.Copy).then_inc(zt_done, 1)

        @block.tensor
        def _(pe):
            pe.wait_ge(ld_lora, 32)
            for k in range(KH):
                if k >= 2:
                    pe.wait_ge(delta_done, k - 1)
                pe.matmul(bank[4 + k % 2][:], lora_bt[:, k * P:(k + 1) * P], lora_a,
                          start=True, stop=True).then_inc(delta_ps, 1)
            pe.wait_ge(sel_done, 1)
            pe.wait_ge(ld_exp, 96)
            for k in range(KH):
                pe.matmul(bank[6][:, k * ZL:k * ZL + ZC], l1a[:, k * P:(k + 1) * P], sel_er[:, 0:ZC],
                          start=True, stop=True)
                pe.matmul(bank[6][:, k * ZL + ZC:(k + 1) * ZL], rw[:, k * P:(k + 1) * P], sel_e[:],
                          start=True, stop=True)
            for i in range(2):
                mm = pe.matmul(bank[6][:, KH * ZL + i * NACT:KH * ZL + (i + 1) * NACT], pr_bc[:, i, :],
                               sel_e[:], start=True, stop=True)
            mm.then_inc(sel_ps, 1)
            pe.wait_ge(iota_done, 8)
            pe.matmul(bank[7][0:ZS, :], sel_er[:], l1b[:], start=True, stop=False)
            pe.matmul(bank[7][0:ZS, :], bias_rows[:], bb[:], start=False, stop=True).then_inc(b_ps, 1)
            pe.wait_ge(diag_done, 2)
            for t in range(NT):
                pe.wait_ge(mask_done, t + 1)
                for k in range(KH):
                    pe.matmul(bank[k][:], diag_h[:, t, :], mask[t % 4][:, k, :], start=(t == 0), stop=False)
                for k in range(KH):
                    mm = pe.matmul(bank[k][:], diag_l[:, t, :], mask[t % 4][:, k, :], start=False,
                                   stop=(t == NT - 1))
                mm.then_inc(mask_used, 1)
            pe.wait_ge(band_done, 2)
            pe.wait_ge(delta_done, KH)
            pe.matmul(bank[4][:, 0:NB], band[:], ymean[:], start=True, stop=True).then_inc(conv_ps, 1)

            def weight_total(i, dst, parts):
                pe.wait_ge(wsum_done[i], parts)
                pe.matmul(dst, ones[:], wsum[:, i, 0:parts], start=True, stop=True).then_inc(wtot_ps, 1)

            weight_total(0, bank[5][:, 0:4], KH)
            pe.wait_ge(weff_done, KH)
            pe.wait_ge(ld_wbase, 16)
            pe.wait_ge(sel_read, 3)
            for k in range(KH):
                for o in range(KH):
                    mm = pe.matmul(bank[k][:], cond[:, o, k * P:(k + 1) * P], wcat[:, o, 0:H],
                                   start=(o == 0), stop=(o == KH - 1))
                mm.then_inc(fold_ps, 1)
                for o in range(KH):
                    mm = pe.matmul(bank[6][:, k * ZL:(k + 1) * ZL], cond[:, o, k * P:(k + 1) * P],
                                   wcat[:, o, H:MC], start=(o == 0), stop=(o == KH - 1))
                if k == KH - 1:
                    mm.then_inc(folds_ps, 1)
            pe.wait_ge(wtot_read, 1)
            weight_total(1, bank[5][:, 4:8], KH)

            def x_transposes(b):
                pe.wait_ge(xq_done, b + 1)
                pe.wait_ge(ident_done, 2)
                if b == 0:
                    pe.wait_ge(ml_done, KH)
                else:
                    pe.wait_ge(xt_done, b)
                if b == 2:
                    pe.wait_ge(wtot_read, 3)
                if b >= 3:
                    pe.wait_ge(zl_done, b - 2)
                for k in range(KH):
                    mm = pe.transpose(bank_xT[:, k * P:(k + 1) * P], xq_b[:, b % 2, k * P:(k + 1) * P],
                                      ident_b[:])
                mm.then_inc(xt_ps, 1)

            def gate_up(b, c):
                n = chunk_no(b, c)
                f0, w = CHUNKS[c]
                if c == 0:
                    pe.wait_ge(xt_done, b + 1)
                if b == 0:
                    pe.wait_ge(tern_out, NC + c + 1)
                if n == 0:
                    pe.wait_ge(wtot_read, 2)
                    pe.wait_ge(yexp_done, 1)
                if n == 1:
                    pe.wait_ge(ml_done, KH + 1)
                    pe.wait_ge(b_done, 1)
                if n >= 2:
                    pe.wait_ge(silu_done, n - 1)
                    pe.wait_ge(hmul_done, n - 1)
                for dst, w_t in ((bank_g[n % 2], tern_g), (bank_u[n % 2], tern_u)):
                    for k in range(KH):
                        mm = pe.matmul(dst[:, 0:w], xq_t[:, b % 2, k, :], w_t[:, k, f0:f0 + w],
                                       start=(k == 0), stop=(k == KH - 1))
                mm.then_inc(gu_ps, 1)

            def hidden_transposes(b):
                pe.wait_ge(hb_done, b + 1)
                for half, (j0, j1) in enumerate(((0, 6), (6, KF))):
                    if b == 0:
                        pe.wait_ge(ml_done, KH)
                    else:
                        pe.wait_ge(ht_done, 3 * (b - 1) + 1 + 2 * half)
                    for j in range(j0, j1):
                        rows = P if j < KF - 1 else FL
                        mm = pe.transpose(bank_hT[half][0:rows, (j - j0) * P:(j - j0 + 1) * P],
                                          h_b[:, b % 2, j * P:j * P + rows], ident_b[:])
                    mm.then_inc(ht_ps, 1)

            def down(b):
                if b == 0:
                    pe.wait_ge(tern_out, 2 * NC + len(DOWN_PARTS))
                    pe.wait_ge(ml_done, KH)
                else:
                    pe.wait_ge(x1l_done, b)
                pe.wait_ge(ht_done, 3 * (b + 1))
                for j in range(KF):
                    rows = P if j < KF - 1 else FL
                    mm = pe.matmul(bank_down[:], h_t[0:rows, b % 2, j, :], tern_d[0:rows, j, :],
                                   start=(j == 0), stop=(j == KF - 1))
                mm.then_inc(down_ps, 1)

            def x1_transposes(b):
                pe.wait_ge(x1_done, b + 1)
                for k in range(KH):
                    mm = pe.transpose(bank_down[:, k * P:(k + 1) * P], xs[:, b, k * P:(k + 1) * P], ident[:])
                mm.then_inc(x1t_ps, 1)

            def three_pass(dst, b, c0, c1, last):
                n = 0
                for k in range(KH):
                    for a, m in ((x1t_h, m_h), (x1t_h, m_l), (x1t_l, m_h)):
                        mm = pe.matmul(dst, a[:, b, k, :], m[:, k, c0:c1], start=(n == 0),
                                       stop=(last and n == 3 * KH - 1))
                        n += 1
                return mm

            def z_logits(b):
                pe.wait_ge(x1l_done, b + 1)
                if b < NB - 1:
                    pe.wait_ge(xt_done, min(b + 3, NB))
                if b > 0:
                    pe.wait_ge(zl_done, b)
                three_pass(bank_zl[:, 0:ZL], b, H, MC, True).then_inc(zl_ps, 1)

            x_transposes(0)
            for b in range(NB + 2):
                if b < NB:
                    gate_up(b, 0)
                if b == 1:
                    pe.wait_ge(xt_done, 2)
                    weight_total(2, bank_zl[:, 0:len(DOWN_PARTS)], len(DOWN_PARTS))
                if b >= 2:
                    x1_transposes(b - 2)
                if b < NB:
                    gate_up(b, 1)
                if b >= 2:
                    z_logits(b - 2)
                if 1 <= b <= NB:
                    hidden_transposes(b - 1)
                if b + 1 < NB:
                    x_transposes(b + 1)
                if b < NB:
                    gate_up(b, 2)
                if 1 <= b <= NB:
                    down(b - 1)

            def layer1(b):
                dst = bank[4 + b % 4]
                if b < 4:
                    pe.wait_ge(silu_done, NC * NB)
                    pe.wait_ge(hmul_done, NC * NB)
                else:
                    pe.wait_ge(res_done, b - 3)
                three_pass(dst[:], b, 0, H, False)

            def experts(b):
                pe.wait_ge(zt_done, b // 4 + 1)
                pe.wait_ge(b_done, 1)
                pe.matmul(bank[4 + b % 4][:], zt[:, b, :], b_stack[:], start=False,
                          stop=True).then_inc(y_ps, 1)

            layer1(0)
            layer1(1)
            pe.wait_ge(zs_done, 1)
            pe.wait_ge(ht_done, 3 * NB)
            for b in range(NB):
                mm = pe.transpose(bank[b // 4][0:ZS, (b % 4) * P:(b % 4 + 1) * P], zstack[:, b, :], ident[:])
                if b % 4 == 3:
                    mm.then_inc(zt_ps, 1)
            for b in range(NB):
                if b + 2 < NB:
                    layer1(b + 2)
                experts(b)

        @block.vector
        def _(dve):
            links = [0]

            def link(ins):
                links[0] += 1
                ins.then_inc(dve_chain, 1)
                dve.wait_ge(dve_chain, links[0])

            dve.memset(wsum[:], 0.0).then_inc(eps_done, 1)
            link(dve.memset(eps12[:], 1e-12))
            dve.wait_ge(iota_done, 1)
            dve.tensor_scalar(ident[:], diff[:], 0.0, None, ALU.is_equal).then_inc(ident_done, 1)
            dve.tensor_scalar(ident_b[:], diff[:], 0.0, None, ALU.is_equal).then_inc(ident_done, 1)

            dve.wait_ge(ld_cb, 16)
            link(dve.tensor_reduce(cbm[:, 0:1], cb[:], AX.X, ALU.max, apply_absolute_value=True))
            link(dve.tensor_scalar(cbm[:, 1:2], cbm[:, 0:1], 1e-8, None, ALU.max))
            link(dve.reciprocal(cbm[:, 2:3], cbm[:, 1:2]))
            link(dve.tensor_scalar(cbn[:], cb[:], cbm[:, 2:3], None, ALU.mult))
            link(dve.tensor_tensor(th[:], cbn[:, 0:NT], cbn[:, 1:NCB], ALU.add))
            dve.tensor_tensor(step[:], cbn[:, 1:NCB], cbn[:, 0:NT], ALU.subtract)
            link(dve.tensor_scalar(th[:], th[:], 0.5, None, ALU.mult))
            def t(i):
                return th[:, i:i + 1]
            link(dve.tensor_tensor(t(1), t(1), t(3), ALU.min))
            link(dve.tensor_tensor(t(5), t(5), t(3), ALU.max))
            link(dve.tensor_tensor(t(0), t(0), t(1), ALU.min))
            link(dve.tensor_tensor(t(6), t(6), t(5), ALU.max))
            link(dve.tensor_scalar(t(2), t(2), t(1), t(3), ALU.max, ALU.min))
            link(dve.tensor_scalar(t(4), t(4), t(3), t(5), ALU.max, ALU.min))
            link(dve.tensor_copy(step_h[:], step[:]))
            link(dve.tensor_tensor(step_l[:], step[:], step_h[:].bitcast(F32), ALU.subtract))
            dve.wait_ge(ident_done, 2)
            ident_rep = ident[:].unsqueeze(1).broadcast_to([P, NT, P])
            dve.tensor_tensor(diag_h[:, 0:NT, :], ident_rep, step_h[:].bitcast(F32).unsqueeze(2).broadcast_to([P, NT, P]),
                              ALU.mult).then_inc(diag_done, 1)
            dve.tensor_tensor(diag_l[:], ident_rep, step_l[:].unsqueeze(2).broadcast_to([P, NT, P]),
                              ALU.mult).then_inc(diag_done, 1)

            dve.wait_ge(ld_act, 16)
            link(dve.tensor_copy(act_f[:], act_i[:]))
            link(dve.tensor_scalar(act_n[:], act_f[:], 0.0, float(NE), ALU.is_lt, ALU.mult))
            link(dve.tensor_tensor(act_f[:], act_f[:], act_n[:], ALU.add))
            link(dve.tensor_scalar(act_f[:], act_f[:], 0.0, float(NE - 1), ALU.max, ALU.min))
            link(dve.tensor_scalar(act8[:], act_f[:], float(RK), None, ALU.mult))
            dve.wait_ge(iota_done, 4)
            act8_rep = act8[:].unsqueeze(2).broadcast_to([P, NACT, RK])
            for i in range(3):
                dve.tensor_tensor(sel_er[:, i * ZC:(i + 1) * ZC].rearrange("p (a r) -> p a r", a=NACT),
                                  pick[:], act8_rep, ALU.is_equal)
            dve.tensor_tensor(sel_e[:], part[0:NE, 0:1].broadcast_to([NE, NACT]), act_f[0:NE, :], ALU.is_equal)
            dve.wait_ge(ld_exp, 96)
            dve.tensor_copy(pr_bc[:], pr[:].unsqueeze(2).broadcast_to([NE, 2, P])).then_inc(sel_done, 1)

            dve.wait_ge(scl_done, 1)
            link(dve.reciprocal(scl_inv[:], scl[:]))
            dve.wait_ge(ld_cond, 16)
            for k in range(KH):
                dve.wait_ge(delta_done, k + 1)
                link(dve.tensor_tensor(cond[:, k, :], cond[:, k, :], delta[:, k, :], ALU.add))
                v = cond[:, k, :].rearrange("p (g i) -> p g i", g=KH)
                link(dve.tensor_tensor(v, v, scl_inv[:, k, :].unsqueeze(2).broadcast_to([P, KH, GROUP]), ALU.mult))
            for i in range(NT):
                if i >= 4:
                    dve.wait_ge(mask_used, i - 3)
                dve.tensor_scalar(mask[i % 4], cond[:], t(i), None, ALU.is_gt).then_inc(mask_done, 1)

            dve.wait_ge(ld_conv, 32)
            dve.wait_ge(iota_done, 5)
            link(dve.tensor_copy(len_f[:], len_i[:]))
            for b in range(NB):
                dve.wait_ge(ld_x[b], 16)
                ins = dve.scalar_tensor_tensor(junk[:], t_iota[:], len_f[:, b:b + 1], xs[:, b, :], ALU.is_lt,
                                               ALU.mult, accum_out=ysum[:, b:b + 1])
                link(ins)
            link(dve.reciprocal(len_r[:], len_f[:]))
            dve.tensor_tensor(ymean[:], ysum[:], len_r[:], ALU.mult).then_inc(band_done, 1)
            dve.tensor_scalar(band[:], diff[:], -2.0, cw[:, 0:1], ALU.is_equal, ALU.mult).then_inc(dve_chain, 1)
            links[0] += 1
            for i in range(1, TAPS):
                link(dve.tensor_scalar(band_t[:], diff[:], float(i - 2), cw[:, i:i + 1], ALU.is_equal, ALU.mult))
                ins = dve.tensor_tensor(band[:], band[:], band_t[:], ALU.add)
                if i < TAPS - 1:
                    link(ins)
                else:
                    ins.then_inc(band_done, 1)

            dve.wait_ge(mask_used, NT)
            for k in range(KH):
                v = cond[:, k, :].rearrange("p (g i) -> p g i", g=KH)
                link(dve.scalar_tensor_tensor(v, bank[k][:].rearrange("p (g i) -> p g i", g=KH), cbn[:, 0:1],
                                              scl[:, k, :].unsqueeze(2).broadcast_to([P, KH, GROUP]),
                                              ALU.add, ALU.mult))
                dve.tensor_tensor(cond[:, k, :], cond[:, k, :], delta[:, k, :], ALU.add).then_inc(weff_done, 1)
            dve.wait_ge(sel_ps, 1)
            sel_v = bank[6][:, 0:KH * ZL].rearrange("p (k c) -> p k c", k=KH)
            dve.tensor_copy(wcat[:, :, H:MC], sel_v).then_inc(sel_read, 1)
            dve.tensor_copy(lg[:, 0:2, :], bank[6][:, KH * ZL:KH * ZL + 2 * NACT]
                            .rearrange("p (i a) -> p i a", i=2)).then_inc(sel_read, 2)

            dve.wait_ge(yexp_done, 1)
            link(dve.tensor_scalar(yexp[:], yexp[:], 1.0, None, ALU.add))
            link(dve.reciprocal(gate[:], yexp[:]))

            def x_scales(b0, b1):
                link(dve.tensor_reduce(rmax[:, b0:b1], xs[:, b0:b1, :], AX.X, ALU.max, apply_absolute_value=True))
                link(dve.tensor_tensor(arow[:, b0:b1], rmax[:, b0:b1], gate[:, b0:b1], ALU.mult))
                link(dve.tensor_scalar(arow[:, b0:b1], arow[:, b0:b1], EPS, None, ALU.max))
                link(dve.reciprocal(qx[:, b0:b1], arow[:, b0:b1]))
                link(dve.tensor_scalar(qx[:, b0:b1], qx[:, b0:b1], QMAX, None, ALU.mult))

            def x_dequant(b0, b1):
                dve.tensor_scalar(s_g[:, b0:b1], arow[:, b0:b1], w127[:, 0:1], None, ALU.mult)
                link(dve.tensor_scalar(s_u[:, b0:b1], arow[:, b0:b1], w127[:, 1:2], None, ALU.mult))

            def x_quantise(b):
                link(dve.tensor_scalar(xq_i[:, b % 2, :], xs[:, b, :], gate[:, b:b + 1], qx[:, b:b + 1],
                                       ALU.mult, ALU.mult))
                if b >= 2:
                    dve.wait_ge(xt_ps, b - 1)
                dve.tensor_copy(xq_b[:, b % 2, :], xq_i[:, b % 2, :]).then_inc(xq_done, 1)

            x_scales(0, 2)
            x_quantise(0)
            x_quantise(1)

            dve.wait_ge(iota_done, 3)
            dve.tensor_scalar(low_row[:], part[:], float(2 * ZC), None, ALU.is_ge)
            link(dve.tensor_scalar(tmp_row[:], part[:], float(3 * ZC), None, ALU.is_equal))
            link(dve.tensor_tensor(low_row[:], low_row[:], tmp_row[:], ALU.subtract))
            link(dve.tensor_scalar(sign_row[:], low_row[:], -2.0, 1.0, ALU.mult, ALU.add))
            link(dve.tensor_scalar(tmp_row[:], part[:], float(3 * ZC), 1.0, ALU.is_lt, ALU.add))
            dve.wait_ge(b_ps, 1)
            link(dve.tensor_scalar(b_full[:], bank[7][0:ZS, :], tmp_row[0:ZS, :], None, ALU.mult))
            link(dve.tensor_copy(b_high[:], b_full[:]))
            link(dve.tensor_scalar(b_full[:], b_full[:], low_row[0:ZS, :], None, ALU.mult))
            dve.scalar_tensor_tensor(b_stack[:], b_high[:].bitcast(F32), sign_row[0:ZS, :], b_full[:],
                                     ALU.mult, ALU.add).then_inc(b_done, 1)
            dve.wait_ge(lp_done, 1)
            link(dve.tensor_tensor(log_prior[:], log_prior[:], lg[:, 1, :], ALU.add))

            def weight_scale(i, src):
                dve.wait_ge(wtot_ps, i + 1)
                dve.tensor_reduce(wtot[:, i:i + 1], src, AX.X, ALU.add).then_inc(wtot_read, 1)
                dve.wait_ge(wtot_read, i + 1)
                link(dve.tensor_scalar(wscale[:, i:i + 1], wtot[:, i:i + 1], 1.0 / NW, EPS, ALU.mult, ALU.max))
                dve.tensor_scalar(w127[:, i:i + 1], wscale[:, i:i + 1], 1.0 / QMAX, None, ALU.mult)
                link(dve.reciprocal(winv[:, i:i + 1], wscale[:, i:i + 1]))

            tern_no = [0]

            def ternary(i, dst, src, rows=P):
                n = src.shape[1] * src.shape[2]
                tmp = tern_i[0:rows, tern_no[0] % 2, 0:n].rearrange("p (k f) -> p k f", k=src.shape[1])
                link(dve.tensor_scalar(tmp, src, winv[0:rows, i:i + 1], None, ALU.mult))
                dve.tensor_scalar(dst, tmp, 1.0, -1.0, ALU.min, ALU.max).then_inc(tern_out, 1)
                tern_no[0] += 1

            weight_scale(0, bank[5][:, 0:4])
            for f0, w in CHUNKS:
                ternary(0, tern_g[:, :, f0:f0 + w], raw_gate[:, :, f0:f0 + w])

            def m_low(k):
                dve.wait_ge(mh_done, k + 1)
                if k < KH:
                    dst, src, high = m_l[:, k, 0:H], bank[k][:], m_h[:, k, 0:H]
                else:
                    src = bank[6][:, 0:KH * ZL].rearrange("p (k c) -> p k c", k=KH)
                    dst, high = m_l[:, :, H:MC], m_h[:, :, H:MC]
                dve.tensor_tensor(dst, src, high.bitcast(F32), ALU.subtract).then_inc(ml_done, 1)

            for k in range(KH + 1):
                m_low(k)
            weight_scale(1, bank[5][:, 4:8])
            x_dequant(0, 2)
            for f0, w in CHUNKS:
                ternary(1, tern_u[:, :, f0:f0 + w], raw_up[:, :, f0:f0 + w])

            def x_evacuate(b):
                dve.wait_ge(xt_ps, b + 1)
                if b >= 2:
                    dve.wait_ge(gu_ps, NC * (b - 1))
                dve.tensor_copy(xq_t[:, b % 2, :, :], bank_xT[:, 0:H].rearrange("p (k e) -> p k e", k=KH))\
                    .then_inc(xt_done, 1)

            def hidden_chunk(b, c):
                n = chunk_no(b, c)
                f0, w = CHUNKS[c]
                dve.wait_ge(silu_done, n + 1)
                if c == 0 and b >= 2:
                    dve.wait_ge(hint_done, b - 1)
                if n == 0:
                    dve.wait_ge(tern_out, 2 * NC)
                hs = hbuf[b % 2][:, f0:f0 + w]
                dve.tensor_tensor(hs, bank_u[n % 2][:, 0:w], silu[:, n % 2, 0:w], ALU.mult)\
                    .then_inc(hmul_done, 1)
                dve.wait_ge(hmul_done, n + 1)
                link(dve.tensor_reduce(hmax[:, b % 2, c:c + 1], hs, AX.X, ALU.max, apply_absolute_value=True))

            def hidden_scale(b):
                o = slice(b, b + 1)
                link(dve.tensor_reduce(hred[:, o], hmax[:, b % 2, :], AX.X, ALU.max))
                link(dve.tensor_scalar(harow[:, o], hred[:, o], s_u[:, o], EPS, ALU.mult, ALU.max))
                link(dve.reciprocal(hrec[:, o], harow[:, o]))
                dve.tensor_scalar(hq[:, o], hrec[:, o], QMAX, s_u[:, o], ALU.mult, ALU.mult)\
                    .then_inc(hscale_done, 1)

            def hidden_bf16(b):
                dve.wait_ge(hint_done, b + 1)
                if b >= 2:
                    dve.wait_ge(ht_ps, 2 * (b - 1))
                dve.tensor_copy(h_b[:, b % 2, :], h_i[:, b % 2, :]).then_inc(hb_done, 1)

            def residual(b):
                o = slice(b, b + 1)
                link(dve.tensor_scalar(s_d[:, o], harow[:, o], w127[:, 2:3], None, ALU.mult))
                dve.wait_ge(down_ps, b + 1)
                dve.scalar_tensor_tensor(xs[:, b, :], bank_down[:], s_d[:, o], xs[:, b, :],
                                         ALU.mult, ALU.add).then_inc(x1_done, 1)

            def x1_low(b):
                dve.wait_ge(x1h_done, b + 1)
                dve.tensor_tensor(x1t_l[:, b, :, :], bank_down[:].rearrange("p (k e) -> p k e", k=KH),
                                  x1t_h[:, b, :, :].bitcast(F32), ALU.subtract).then_inc(x1l_done, 1)

            def zl_copy(b):
                dve.wait_ge(zl_ps, b + 1)
                dve.tensor_copy(zl[:, b, :], bank_zl[:, 0:ZL]).then_inc(zl_done, 1)

            x_evacuate(0)
            for b in range(NB + 2):
                if b < NB:
                    hidden_chunk(b, 0)
                if 1 <= b <= NB:
                    hidden_bf16(b - 1)
                if b == 1:
                    weight_scale(2, bank_zl[:, 0:len(DOWN_PARTS)])
                    for j0, n, rows in DOWN_PARTS:
                        ternary(2, tern_d[0:rows, j0:j0 + n, :], raw_down[0:rows, j0:j0 + n, :], rows)
                if b >= 2:
                    x1_low(b - 2)
                if b < NB:
                    hidden_chunk(b, 1)
                if b >= 2:
                    zl_copy(b - 2)
                if b + 1 < NB:
                    x_evacuate(b + 1)
                if b < NB:
                    hidden_chunk(b, 2)
                    hidden_scale(b)
                if 1 <= b <= NB:
                    residual(b - 1)
                if b + 2 < NB:
                    if b % 2 == 0:
                        x_scales(b + 2, b + 4)
                        x_dequant(b + 2, b + 4)
                    x_quantise(b + 2)

            dve.wait_ge(zl_done, NB)
            link(dve.tensor_tensor(lg[:], zl[:, :, ZC:ZL], log_prior[:].unsqueeze(1).broadcast_to([P, NB, NACT]),
                                   ALU.add))
            link(dve.tensor_reduce(lmax[:], lg[:], AX.X, ALU.max))
            dve.tensor_tensor(lg[:], lg[:], lmax[:].unsqueeze(2).broadcast_to([P, NB, NACT]),
                              ALU.subtract).then_inc(lmax_done, 1)
            dve.wait_ge(ex_done, 1)
            link(dve.tensor_reduce(esum[:], ex[:], AX.X, ALU.add))
            link(dve.reciprocal(esum[:], esum[:]))
            link(dve.tensor_tensor(alpha[:], ex[:], esum[:].unsqueeze(2).broadcast_to([P, NB, NACT]), ALU.mult))
            for a in range(NACT):
                ins = dve.tensor_tensor(zz[:, :, a * RK:(a + 1) * RK], zl[:, :, a * RK:(a + 1) * RK],
                                        alpha[:, :, a:a + 1].broadcast_to([P, NB, RK]), ALU.mult)
            link(ins)
            link(dve.tensor_copy(zz_h[:], zz[:]))
            dve.memset(zstack[:, :, 3 * ZC:ZS], 1.0)
            high = zz_h[:].bitcast(F32)
            dve.tensor_copy(zstack[:, :, 0:ZC], high)
            dve.tensor_copy(zstack[:, :, 2 * ZC:3 * ZC], high)
            dve.tensor_tensor(zstack[:, :, ZC:2 * ZC], zz[:], high, ALU.subtract).then_inc(zs_done, 1)
            for b in range(NB):
                dve.wait_ge(y_ps, b + 1)
                if b >= 2:
                    dve.wait_ge(stored[b % 2], 16 * (b // 2))
                dve.tensor_tensor(res[:, b % 2, :], bank[4 + b % 4][:], xs[:, b, :], ALU.add)\
                    .then_inc(res_done, 1)


def kernel(x, itok_B_9_3973, condB_codebook, L0_cond_conv_w, L0_ffn_w_gate, L0_ffn_w_up, L0_ffn_w_down,
           L1_cond_weight, L1_cond_scale_log, L1_cond_lora_A, L1_cond_lora_B, L1_ffn_W_base, L1_ffn_b_base,
           L1_ffn_lora_A, L1_ffn_lora_B, L1_ffn_router_W, L1_ffn_router_b, L1_ffn_domain_prior, L1_ffn_active):
    import numpy as np
    import concourse.bacc as bacc
    from concourse.bass_utils import run_bass_kernel_spmd

    n = np.asarray
    layout = {
        "x": n(x),
        "length": n(itok_B_9_3973),
        "codebook": n(condB_codebook),
        "conv_w": n(L0_cond_conv_w).reshape(TAPS),
        "w_gate_t": n(L0_ffn_w_gate).T,
        "w_up_t": n(L0_ffn_w_up).T,
        "w_down_t": n(L0_ffn_w_down).T,
        "cond_w": n(L1_cond_weight),
        "scale_log": n(L1_cond_scale_log),
        "lora0_a": n(L1_cond_lora_A),
        "lora0_b_t": n(L1_cond_lora_B).T,
        "w_base_t": n(L1_ffn_W_base).T,
        "b_base": n(L1_ffn_b_base).reshape(1, H),
        "lora1_a": n(L1_ffn_lora_A).reshape(NE * RK, H),
        "lora1_b_t": n(L1_ffn_lora_B).transpose(0, 2, 1).reshape(NE * RK, H),
        "router_w": n(L1_ffn_router_W),
        "router_b": n(L1_ffn_router_b).reshape(NE, 1),
        "prior": n(L1_ffn_domain_prior).reshape(NE, 1),
        "active": n(L1_ffn_active),
    }
    nc = bacc.Bacc("TRN2", target_bir_lowering=False, num_devices=1)
    arrays, args = {}, {}
    for name, a in layout.items():
        a = np.ascontiguousarray(a)
        arrays[f"in_{name}"] = a
        args[name] = nc.dram_tensor(f"in_{name}", a.shape, mybir.dt.from_np(a.dtype), kind="ExternalInput").ap()
    args["out"] = nc.dram_tensor("out_x", (NB, E, H), F32, kind="ExternalOutput").ap()
    build(nc, **args)
    r = run_bass_kernel_spmd(nc, [arrays], core_ids=[0])
    return r.results[0]["out_x"]
```

```python
from contextlib import ExitStack

import concourse.bass as bass
from concourse import mybir

F32 = mybir.dt.float32
F32R = mybir.dt.float32r
BF16 = mybir.dt.bfloat16
I16 = mybir.dt.int16
I32 = mybir.dt.int32
ALU = mybir.AluOpType
ACT = mybir.ActivationFunctionType
AX = mybir.AxisListType

P = 128
NB, E, H = 8, 128, 512
F = 1376
KH = H // P
KF = -(-F // P)
FL = F - (KF - 1) * P
CHUNKS = [(0, 464), (464, 464), (928, 448)]
NC = len(CHUNKS)
NCB = 8
NT = NCB - 1
GROUP = 128
RANK0 = 64
LORA0_FACTOR = 32.0 / RANK0
NE, NACT, RK = 16, 4, 8
ZC = NACT * RK
ZL = ZC + NACT
MC = H + ZL
ZS = 3 * ZC + 2
TAPS = 5
SMALL = NCB + TAPS + NB + NACT
NW = float(F * H)
QMAX = 127.0
EPS = 1e-5
WARM_UP = 3
UP_ROUNDED_BY_ACT = 1
DOWN_PARTS = [(0, 3, P), (3, 3, P), (6, 2, P), (8, 2, P), (KF - 1, 1, FL)]


def build(nc, x, small, w_gate_t, w_up_t, w_down_t, cond_w, scale_log, lora0, w_base_t, b_base,
          lora1, router, out):
    with ExitStack() as ctx:
        def sb(name, shape, dt=F32):
            return ctx.enter_context(nc.sbuf_tensor(name, shape, dt))

        def sem(name):
            return ctx.enter_context(nc.semaphore(name))

        bank = [ctx.enter_context(nc.psum_tensor(f"bank{i}", [P, 512], F32)) for i in range(8)]
        bank_hT = [bank[0][:].bitcast(BF16), bank[1][:].bitcast(BF16)]
        bank_down = bank[2]
        bank_xT = bank[3][:].bitcast(BF16)
        bank_zt = [bank[3], bank[1]]
        bank_zr = bank[0]
        bank_zs = [bank[3], bank[1]]
        bank_m = [bank[7], bank[6], bank[0], bank[1]]
        bank_ms = bank[2]
        bank_delta = bank[0:4]
        bank_cb = bank[4:8]
        bank_sel = bank[0]
        bank_b = bank[1]
        bank_conv = bank[3][:, 0:NB]
        bank_total = [bank[3][:, NB:NB + KH], bank[5][:, 0:KH], bank[5][:, KH:KH + len(DOWN_PARTS)]]
        bank_warm = bank[7]
        bank_g = [bank[4], bank[6]]
        bank_u = [bank[5], bank[7]]
        bank_y = [bank[i] for i in (4, 5, 6, 7, 2, 0, 4, 5)]

        xs = sb("xs", [P, NB, H])
        raw = [sb("raw_gate_down", [P, KF * H]), sb("raw_up", [P, KH * F])]
        raw_gate = raw[0][:, 0:KH * F].rearrange("p (k f) -> p k f", k=KH)
        raw_up = raw[1][:, :].rearrange("p (k f) -> p k f", k=KH)
        raw_down = raw[0][:, :].rearrange("p (j h) -> p j h", j=KF)
        cond = sb("cond", [P, KH, H])
        wcat = sb("wcat", [P, KH, MC])
        lora_sb = sb("lora_sb", [P, 2, H])
        lora_a, lora_bt = lora_sb[0:RANK0, 0, :], lora_sb[0:RANK0, 1, :]
        slog = sb("slog", [P, KH, KH])
        small_sb = sb("small_sb", [P, SMALL])
        cb = small_sb[:, 0:NCB]
        cw = small_sb[:, NCB:NCB + TAPS]
        len_i = small_sb[:, NCB + TAPS:NCB + TAPS + NB].bitcast(I32)
        act_i = small_sb[:, NCB + TAPS + NB:SMALL].bitcast(I32)
        l1ab = sb("l1ab", [NE * RK, 2, H])
        l1a, l1b = l1ab[:, 0, :], l1ab[:, 1, :]
        rwp = sb("rwp", [NE, H + 2])
        rw, pr = rwp[:, 0:H], rwp[:, H:H + 2]
        bb = sb("bb", [1, H])

        t_iota = sb("t_iota", [P, H])
        diff = sb("diff", [P, P])
        pick = sb("pick", [P, NACT, RK])
        part = sb("part", [P, 1])
        ident = sb("ident", [P, P])
        ident_b = sb("ident_b", [P, P], BF16)
        ones = sb("ones", [P, P])
        bias_rows = sb("bias_rows", [1, ZS])
        low_row = sb("low_row", [P, 1])
        sign_row = sb("sign_row", [P, 1])
        tmp_row = sb("tmp_row", [P, 1])
        two_row = sb("two_row", [P, 1])

        cbm = sb("cbm", [P, 4])
        cbn = sb("cbn", [P, NCB])
        th = sb("th", [P, NT])
        step = sb("step", [P, NT])
        step_h = sb("step_h", [P, NT], F32R)
        step_l = sb("step_l", [P, NT])
        diag_h = sb("diag_h", [P, NB, P], F32R)
        diag_l = sb("diag_l", [P, NT, P], F32R)
        scl = sb("scl", [P, KH, KH])
        scl_inv = sb("scl_inv", [P, KH, KH])
        delta = sb("delta", [P, KH, H])
        fr = sb("fr", [P, 4, KH * H], F32R)
        mask = [fr[:, i, :].rearrange("p (k h) -> p k h", k=KH) for i in range(4)]
        x1t_h = fr[:, 0:2, :].rearrange("p a (b k e) -> p (a b) k e", b=4, k=KH)
        x1t_l = fr[:, 2:4, :].rearrange("p a (b k e) -> p (a b) k e", b=4, k=KH)

        table_use = sb("table_use", [P, 1])
        junk = sb("junk", [P, H])
        act_f = sb("act_f", [P, NACT])
        act_n = sb("act_n", [P, NACT])
        act8 = sb("act8", [P, NACT])
        sel_er = sb("sel_er", [P, ZS])
        sel_e = sb("sel_e", [NE, NACT])
        pr_bc = sb("pr_bc", [NE, 2, P])
        log_prior = sb("log_prior", [P, NACT])
        eps12 = sb("eps12", [P, 1])
        b_full = sb("b_full", [ZS, H])
        b_high = fr[0:ZS, 3, 3 * H:4 * H]
        b_stack = sb("b_stack", [ZS, H], F32R)

        len_f = sb("len_f", [P, NB])
        len_r = sb("len_r", [P, NB])
        ysum = sb("ysum", [P, NB])
        ymean = sb("ymean", [P, NB])
        band = sb("band", [P, P])
        band_t = sb("band_t", [P, P])
        yexp = sb("yexp", [P, NB])
        gate = sb("gate", [P, NB])
        rmax = sb("rmax", [P, NB])
        arow = sb("arow", [P, NB])
        qx = sb("qx", [P, NB])
        s_g = sb("s_g", [P, NB])
        s_u = sb("s_u", [P, NB])
        wsum = sb("wsum", [P, 3, len(DOWN_PARTS)])
        wtot = sb("wtot", [P, 3])
        wscale = sb("wscale", [P, 3])
        winv = sb("winv", [P, 3])
        w127 = sb("w127", [P, 3])
        tern_g = sb("tern_g", [P, KH, F], BF16)
        tern_u = sb("tern_u", [P, KH, F], BF16)
        tern_d = sb("tern_d", [P, KF, H], BF16)
        junk_a = tern_d[:].rearrange("p j h -> p (j h)")[:, 0:4 * H]
        tern_i = sb("tern_i", [P, 2, KH * CHUNKS[0][1]], I16)
        xq_i = lora_sb[:, 0, :].bitcast(I16).rearrange("p (i h) -> p i h", i=2)
        xq_b = lora_sb[:, 1, :].bitcast(BF16).rearrange("p (i h) -> p i h", i=2)
        xq_t = l1a.bitcast(BF16).rearrange("p (i k e) -> p i k e", i=2, k=KH)
        cond_flat = cond[:].rearrange("p k h -> p (k h)")
        silu = cond_flat[:, 0:2 * CHUNKS[0][1]].rearrange("p (i f) -> p i f", i=2)
        hbuf = [raw[1][:, i * F:(i + 1) * F] for i in range(2)]
        h_i = raw[1][:, 2 * F:3 * F].bitcast(I16).rearrange("p (i f) -> p i f", i=2)
        h_b = raw[1][:, 3 * F:4 * F].bitcast(BF16).rearrange("p (i f) -> p i f", i=2)
        hmax = sb("hmax", [P, 2, NC])
        hred = sb("hred", [P, NB])
        harow = sb("harow", [P, NB])
        hrec = sb("hrec", [P, NB])
        hq = sb("hq", [P, NB])
        s_d = sb("s_d", [P, NB])
        h_t = delta[:].rearrange("p k h -> p (k h)")[:, 0:KF * P].bitcast(BF16)\
            .rearrange("p (i j e) -> p i j e", i=2, j=KF)

        m_h = sb("m_h", [P, KH, MC], F32R)
        m_l = sb("m_l", [P, KH, MC], F32R)
        wcat_flat = wcat[:].rearrange("p k c -> p (k c)")
        zstack = wcat_flat[:, 0:NB * ZS].rearrange("p (b c) -> p b c", b=NB)
        zlt = raw[1][0:ZL, 0:NB * P]
        zl = wcat_flat[:, NB * ZS:NB * (ZS + ZL)].rearrange("p (b c) -> p b c", b=NB)
        zz = wcat_flat[:, NB * (ZS + ZL):NB * (ZS + ZL + ZC)].rearrange("p (b c) -> p b c", b=NB)
        lg = sb("lg", [P, NB, NACT])
        lmax = sb("lmax", [P, NB])
        ex = sb("ex", [P, NB, NACT])
        esum = sb("esum", [P, NB])
        alpha = sb("alpha", [P, NB, NACT])
        zz_h = diag_l[:].rearrange("p t c -> p (t c)")[:, 0:NB * ZC].rearrange("p (b c) -> p b c", b=NB)
        zt = diag_h[0:ZS, :, :]

        ld_small, ld_lora, ld_slog, ld_exp = sem("ld_small"), sem("ld_lora"), sem("ld_slog"), sem("ld_exp")
        ld_cond = [sem(f"ld_cond{k}") for k in range(KH)]
        ld_wbase = sem("ld_wbase")
        ld_x = [sem(f"ld_x{b}") for b in range(NB)]
        ld_gate = [sem(f"ld_gate{k}") for k in range(KH)]
        ld_up = [sem(f"ld_up{k}") for k in range(KH)]
        ld_down = [sem(f"ld_down{i}") for i in range(len(DOWN_PARTS))]
        stored = sem("stored")
        iota_done = sem("iota_done")
        ident_done = sem("ident_done")
        eps_done = sem("eps_done")
        lora_scaled = sem("lora_scaled")
        delta_ps = sem("delta_ps")
        norm_step = sem("norm_step")
        norm_done = sem("norm_done")
        step_done = sem("step_done")
        b_full_done = sem("b_full_done")
        rows_done = sem("rows_done")
        delta_done = sem("delta_done")
        scl_done = sem("scl_done")
        diag_done = sem("diag_done")
        sel_done = sem("sel_done")
        sel_ps = sem("sel_ps")
        sel_read = sem("sel_read")
        b_ps = sem("b_ps")
        b_done = sem("b_done")
        lp_done = sem("lp_done")
        mask_done = sem("mask_done")
        mask_used = sem("mask_used")
        cb_ps = sem("cb_ps")
        value_done = sem("value_done")
        weff_done = sem("weff_done")
        band_done = sem("band_done")
        band_step = sem("band_step")
        ymean_done = sem("ymean_done")
        conv_ps = sem("conv_ps")
        yexp_done = sem("yexp_done")
        wsum_done = [sem("gsum_done"), sem("usum_done"), sem("dsum_done")]
        wtot_ps = sem("wtot_ps")
        wtot_read = sem("wtot_read")
        winv_done = sem("winv_done")
        tern_int = sem("tern_int")
        tern_out = sem("tern_out")
        fold_ps = sem("fold_ps")
        folds_ps = sem("folds_ps")
        mh_done = sem("mh_done")
        ml_done = sem("ml_done")
        xq_done = sem("xq_done")
        xt_ps = sem("xt_ps")
        xt_done = sem("xt_done")
        gu_ps = sem("gu_ps")
        silu_done = sem("silu_done")
        hmul_done = sem("hmul_done")
        hscale_done = sem("hscale_done")
        hint_done = sem("hint_done")
        hb_done = sem("hb_done")
        ht_ps = sem("ht_ps")
        ht_done = sem("ht_done")
        down_ps = sem("down_ps")
        x1_done = sem("x1_done")
        x1t_ps = sem("x1t_ps")
        x1h_done = sem("x1h_done")
        x1l_done = sem("x1l_done")
        zlt_ps = sem("zlt_ps")
        zlt_done = sem("zlt_done")
        zl_ps = sem("zl_ps")
        lmax_done = sem("lmax_done")
        ex_done = sem("ex_done")
        zs_done = sem("zs_done")
        zt_ps = sem("zt_ps")
        zt_done = sem("zt_done")
        y_ps = sem("y_ps")
        res_done = sem("res_done")
        dve_chain = sem("dve_chain")

        def chunk_no(b, c):
            return NC * b + c

        block = ctx.enter_context(nc.Block())

        @block.sync
        def _(sp):
            cond_v = cond_w.rearrange("(k p) h -> p k h", p=P)
            for k in range(KH):
                sp.dma_start(cond[:, k, :], cond_v[:, k, :]).then_inc(ld_cond[k], 16)
            sp.dma_start(l1ab[:], lora1).then_inc(ld_exp, 16)
            sp.dma_start(rwp[:], router).then_inc(ld_exp, 16)
            sp.dma_start(bb[:], b_base).then_inc(ld_exp, 16)
            for b in range(NB):
                sp.dma_start(xs[:, b, :], x[b]).then_inc(ld_x[b], 16)
            gate_v = w_gate_t.rearrange("(k p) f -> p k f", p=P)
            up_v = w_up_t.rearrange("(k p) f -> p k f", p=P)
            for k in range(KH):
                sp.dma_start(raw_gate[:, k, :], gate_v[:, k, :]).then_inc(ld_gate[k], 16)
            sp.dma_start(wcat[:, :, 0:H], w_base_t.rearrange("(k p) c -> p k c", p=P)).then_inc(ld_wbase, 16)
            for k in range(KH):
                sp.dma_start(raw_up[:, k, :], up_v[:, k, :]).then_inc(ld_up[k], 16)
            sp.wait_ge(tern_out, NC)
            for i, (j0, n, rows) in enumerate(DOWN_PARTS):
                src = w_down_t[j0 * P:j0 * P + (n - 1) * P + rows, :].rearrange("(j p) h -> p j h", p=rows)
                sp.dma_start(raw_down[0:rows, j0:j0 + n, :], src).then_inc(ld_down[i], 16)
            for b in range(NB):
                sp.wait_ge(res_done, b + 1)
                sp.dma_start(out[b], xs[:, b, :]).then_inc(stored, 16)
            sp.wait_ge(stored, 16 * NB)

        @block.gpsimd
        def _(pool):
            pool.iota(diff[:], [[-1, P]], 0, 1, allow_small_or_imprecise_dtypes=True).then_inc(iota_done, 1)
            pool.iota(pick[:], [[0, NACT], [-1, RK]], 0, 1, allow_small_or_imprecise_dtypes=True).then_inc(iota_done, 1)
            pool.iota(part[:], [[0, 1]], 0, 1, allow_small_or_imprecise_dtypes=True).then_inc(iota_done, 1)
            pool.memset(sel_er[:], 0.0).then_inc(iota_done, 1)
            pool.iota(t_iota[:], [[1, H]], 0, 0, allow_small_or_imprecise_dtypes=True).then_inc(iota_done, 1)
            pool.memset(ones[:], 1.0).then_inc(iota_done, 1)
            pool.memset(bias_rows[:], 1.0).then_inc(iota_done, 1)
            pool.wait_ge(iota_done, 7)
            pool.memset(bias_rows[:, 0:3 * ZC], 0.0).then_inc(iota_done, 2)

            pool.tensor_scalar(low_row[:], part[:], float(2 * ZC), None, ALU.is_ge).then_inc(rows_done, 1)
            pool.tensor_scalar(tmp_row[:], part[:], float(3 * ZC), None, ALU.is_equal).then_inc(rows_done, 1)
            pool.wait_ge(rows_done, 2)
            pool.tensor_tensor(low_row[:], low_row[:], tmp_row[:], ALU.subtract).then_inc(rows_done, 1)
            pool.wait_ge(rows_done, 3)
            pool.tensor_scalar(sign_row[:], low_row[:], -2.0, 1.0, ALU.mult, ALU.add).then_inc(rows_done, 1)
            pool.tensor_scalar(two_row[:], part[:], float(3 * ZC), 1.0, ALU.is_lt, ALU.add).then_inc(rows_done, 1)

            for k in range(0, KH, 2):
                pool.wait_ge(norm_step, k + 1)
                v = cond[:, k, :].rearrange("p (g i) -> p g i", g=KH)
                pool.tensor_tensor(v, v, scl_inv[:, k, :].unsqueeze(2).broadcast_to([P, KH, GROUP]),
                                   ALU.mult).then_inc(norm_done, 1)

            pool.wait_ge(ld_small, 16)
            pool.tensor_scalar(band[:], diff[:], -2.0, cw[:, 0:1], ALU.is_equal, ALU.mult).then_inc(band_step, 1)
            for i in range(1, TAPS):
                pool.tensor_scalar(band_t[:], diff[:], float(i - 2), cw[:, i:i + 1], ALU.is_equal,
                                   ALU.mult).then_inc(band_step, 1)
                pool.wait_ge(band_step, 2 * i)
                pool.tensor_tensor(band[:], band[:], band_t[:], ALU.add)\
                    .then_inc(band_step if i < TAPS - 1 else band_done, 1)
                if i < TAPS - 1:
                    pool.wait_ge(band_step, 2 * i + 1)

            pool.wait_ge(delta_done, KH)
            for k in range(0, KH, 2):
                pool.wait_ge(value_done, k + 1)
                pool.tensor_tensor(cond[:, k, :], cond[:, k, :], delta[:, k, :], ALU.add).then_inc(weff_done, 1)

        @block.scalar
        def _(act):
            act.dma_start(small_sb[:], small.partition_broadcast(P)).then_inc(ld_small, 16)
            act.dma_start(lora_sb[0:RANK0, :, :], lora0).then_inc(ld_lora, 16)
            act.dma_start(slog[:], scale_log).then_inc(ld_slog, 16)

            act.wait_ge(iota_done, 3)
            act.activation(table_use[:], part[:], ACT.Exp, scale=0.0)
            act.wait_ge(ld_lora, 16)
            act.activation(lora_a, lora_a, ACT.Copy, scale=LORA0_FACTOR).then_inc(lora_scaled, 1)

            def diagonals(i):
                act.activation(diag_h[:, i, :], ident[:], ACT.Copy,
                               scale=step_h[:, i:i + 1].bitcast(F32)).then_inc(diag_done, 1)
                act.activation(diag_l[:, i, :], ident[:], ACT.Copy, scale=step_l[:, i:i + 1]).then_inc(diag_done, 1)

            act.wait_ge(ident_done, 2)
            act.wait_ge(step_done, 1)
            diagonals(0)
            act.wait_ge(ld_slog, 16)
            act.activation(scl[:], slog[:], ACT.Exp).then_inc(scl_done, 1)
            diagonals(1)
            for k in range(KH):
                act.wait_ge(norm_step, k + 1)
                act.activation(delta[:, k, :], bank_delta[k][:], ACT.Copy).then_inc(delta_done, 1)
            for i in range(2, NT):
                diagonals(i)

            def weight_sum(i, k, src, rows=P):
                n = src.shape[1] * (src.shape[2] if len(src.shape) > 2 else 1)
                dst = junk_a[0:rows, 0:n]
                if k > 0:
                    act.wait_ge(wsum_done[i], k)
                elif i > 0:
                    act.wait_ge(wsum_done[i - 1], KH)
                if len(src.shape) > 2:
                    dst = dst.rearrange("p (j h) -> p j h", j=src.shape[1])
                act.activation(dst, src, ACT.Abs, accum_out=wsum[0:rows, i, k:k + 1]).then_inc(wsum_done[i], 1)

            act.wait_ge(eps_done, 1)
            for k in range(KH):
                act.wait_ge(ld_gate[k], 16)
                weight_sum(0, k, raw_gate[:, k, :])
            for k in range(KH):
                act.wait_ge(ld_up[k], 16)
                weight_sum(1, k, raw_up[:, k, :])
            act.wait_ge(b_ps, 1)
            act.wait_ge(rows_done, 5)
            act.activation(b_full[:], bank_b[0:ZS, :], ACT.Copy, scale=two_row[0:ZS, :]).then_inc(b_full_done, 1)

            def m_high(k):
                act.wait_ge(fold_ps, k + 1)
                act.activation(m_h[:, k, 0:H], bank_m[k][:], ACT.Copy).then_inc(mh_done, 1)

            act.wait_ge(winv_done, 2)
            act.wait_ge(tern_out, NC)
            f0, w = CHUNKS[UP_ROUNDED_BY_ACT]
            act.activation(tern_i[:, UP_ROUNDED_BY_ACT % 2, 0:KH * w].rearrange("p (k f) -> p k f", k=KH),
                           raw_up[:, :, f0:f0 + w], ACT.Copy, scale=winv[:, 1:2]).then_inc(tern_int, 1)
            for i, (j0, n, rows) in enumerate(DOWN_PARTS):
                act.wait_ge(ld_down[i], 16)
                weight_sum(2, i, raw_down[0:rows, j0:j0 + n, :], rows)
                if i == 1:
                    m_high(0)
                    act.wait_ge(conv_ps, 1)
                    act.activation(yexp[:], bank_conv, ACT.Exp, scale=-1.0).then_inc(yexp_done, 1)
            act.wait_ge(sel_read, 2)
            act.activation(log_prior[:], lg[:, 0, :], ACT.Ln, bias=eps12[:, 0:1]).then_inc(lp_done, 1)
            m_high(1)
            m_high(2)
            act.wait_ge(winv_done, 3)
            for i, (j0, n, rows) in enumerate(DOWN_PARTS):
                if i % 2 == 0:
                    act.wait_ge(tern_out, 2 * NC + max(i - 1, 0))
                    act.activation(tern_i[0:rows, 0, 0:n * H].rearrange("p (k f) -> p k f", k=n),
                                   raw_down[0:rows, j0:j0 + n, :], ACT.Copy,
                                   scale=winv[0:rows, 2:3]).then_inc(tern_int, 1)

            def x_evacuate(b):
                act.wait_ge(xt_ps, b + 1)
                if b >= 2:
                    act.wait_ge(gu_ps, NC * (b - 1))
                act.activation(xq_t[:, b % 2, :, :], bank_xT[:, 0:H].rearrange("p (k e) -> p k e", k=KH),
                               ACT.Copy).then_inc(xt_done, 1)

            def silu_chunk(b, c):
                n = chunk_no(b, c)
                w = CHUNKS[c][1]
                act.wait_ge(gu_ps, n + 1)
                if n >= 2:
                    act.wait_ge(hmul_done, n - 1)
                act.activation(silu[:, n % 2, 0:w], bank_g[n % 2][:, 0:w], ACT.Silu,
                               scale=s_g[:, b:b + 1]).then_inc(silu_done, 1)

            def hidden_round(b):
                act.wait_ge(hscale_done, b + 1)
                if b >= 2:
                    act.wait_ge(hb_done, b - 1)
                act.activation(h_i[:, b % 2, :], hbuf[b % 2], ACT.Copy,
                               scale=hq[:, b:b + 1]).then_inc(hint_done, 1)

            def hidden_evacuate(b):
                for half, (j0, j1) in enumerate(((0, 6), (6, KF - 1))):
                    act.wait_ge(ht_ps, 2 * b + half + 1)
                    if b >= 2 and half == 0:
                        act.wait_ge(down_ps, b - 1)
                    src = bank_hT[half]
                    if half == 1:
                        act.activation(h_t[0:FL, b % 2, KF - 1, :], src[0:FL, (j1 - j0) * P:(j1 - j0 + 1) * P],
                                       ACT.Copy).then_inc(ht_done, 1)
                    act.activation(h_t[:, b % 2, j0:j1, :],
                                   src[:, 0:(j1 - j0) * P].rearrange("p (j e) -> p j e", e=P),
                                   ACT.Copy).then_inc(ht_done, 1)

            def x1_high(b):
                act.wait_ge(x1t_ps, b + 1)
                act.activation(x1t_h[:, b, :, :], bank_down[:].rearrange("p (k e) -> p k e", k=KH),
                               ACT.Copy).then_inc(x1h_done, 1)

            x_evacuate(0)
            for b in range(NB + 2):
                if b < NB:
                    silu_chunk(b, 0)
                if b >= 2:
                    x1_high(b - 2)
                if b == 0:
                    m_high(3)
                    act.wait_ge(folds_ps, 1)
                    act.activation(m_h[:, :, H:MC], bank_ms[:, 0:KH * ZL].rearrange("p (k c) -> p k c", k=KH),
                                   ACT.Copy).then_inc(mh_done, 1)
                if b < NB:
                    silu_chunk(b, 1)
                if 1 <= b <= NB:
                    hidden_evacuate(b - 1)
                if b + 1 < NB:
                    x_evacuate(b + 1)
                if b < NB:
                    silu_chunk(b, 2)
                    hidden_round(b)
            for half in range(2):
                act.wait_ge(zlt_ps, half + 1)
                act.activation(zlt[:, 4 * half * P:4 * (half + 1) * P], bank_zt[half][0:ZL, :],
                               ACT.Copy).then_inc(zlt_done, 1)
            act.wait_ge(lmax_done, 1)
            act.activation(ex[:], lg[:], ACT.Exp).then_inc(ex_done, 1)
            for i in range(2):
                act.wait_ge(zt_ps, i + 1)
                act.activation(zt[:, 4 * i:4 * i + 4, :], bank_zs[i][0:ZS, :].rearrange("p (b e) -> p b e", b=4),
                               ACT.Copy).then_inc(zt_done, 1)

        @block.tensor
        def _(pe):
            def keep_clock(n):
                for i in range(n):
                    pe.matmul(bank_warm[:], ident[:], t_iota[:], start=True, stop=True)

            pe.wait_ge(ident_done, 2)
            pe.wait_ge(iota_done, 6)
            keep_clock(WARM_UP)
            pe.wait_ge(lora_scaled, 1)
            for k in range(KH):
                pe.matmul(bank_delta[k][:], lora_bt[:, k * P:(k + 1) * P], lora_a,
                          start=True, stop=True).then_inc(delta_ps, 1)
            keep_clock(WARM_UP)

            def weight_total(i, dst, parts):
                pe.wait_ge(wsum_done[i], parts)
                pe.matmul(dst, ones[:], wsum[:, i, 0:parts], start=True, stop=True).then_inc(wtot_ps, 1)

            for t in range(NT):
                pe.wait_ge(diag_done, 2 * (t + 1))
                pe.wait_ge(mask_done, t + 1)
                for k in range(KH):
                    pe.matmul(bank_cb[k][:], diag_h[:, t, :], mask[t % 4][:, k, :], start=(t == 0), stop=False)
                    mm = pe.matmul(bank_cb[k][:], diag_l[:, t, :], mask[t % 4][:, k, :], start=False,
                                   stop=(t == NT - 1))
                    if t == NT - 1:
                        mm.then_inc(cb_ps, 1)
                    elif k == KH - 1:
                        mm.then_inc(mask_used, 1)
                if t == NT - 2:
                    pe.wait_ge(delta_done, KH)
                    weight_total(0, bank_total[0], KH)
            pe.wait_ge(sel_done, 2)
            pe.wait_ge(ld_exp, 48)
            pe.wait_ge(delta_done, 1)
            for k in range(KH):
                pe.matmul(bank_sel[:, k * ZL:k * ZL + ZC], l1a[:, k * P:(k + 1) * P], sel_er[:, 0:ZC],
                          start=True, stop=True)
                pe.matmul(bank_sel[:, k * ZL + ZC:(k + 1) * ZL], rw[:, k * P:(k + 1) * P], sel_e[:],
                          start=True, stop=True)
            for i in range(2):
                mm = pe.matmul(bank_sel[:, KH * ZL + i * NACT:KH * ZL + (i + 1) * NACT], pr_bc[:, i, :],
                               sel_e[:], start=True, stop=True)
            mm.then_inc(sel_ps, 1)
            pe.wait_ge(iota_done, 9)
            pe.wait_ge(delta_done, 2)
            pe.matmul(bank_b[0:ZS, :], sel_er[:], l1b, start=True, stop=False)
            pe.matmul(bank_b[0:ZS, :], bias_rows[:], bb[:], start=False, stop=True).then_inc(b_ps, 1)

            def conv():
                pe.wait_ge(band_done, 1)
                pe.wait_ge(ymean_done, 1)
                pe.wait_ge(wtot_read, 1)
                pe.matmul(bank_conv, band[:], ymean[:], start=True, stop=True).then_inc(conv_ps, 1)

            def x_transposes(b):
                pe.wait_ge(xq_done, b + 1)
                pe.wait_ge(ident_done, 2)
                if b == 0:
                    pe.wait_ge(yexp_done, 1)
                else:
                    pe.wait_ge(xt_done, b)
                for k in range(KH):
                    mm = pe.transpose(bank_xT[:, k * P:(k + 1) * P], xq_b[:, b % 2, k * P:(k + 1) * P],
                                      ident_b[:])
                mm.then_inc(xt_ps, 1)

            pe.wait_ge(weff_done, KH)
            weight_total(1, bank_total[1], KH)
            pe.wait_ge(ld_wbase, 16)
            pe.wait_ge(sel_read, 3)
            pe.wait_ge(b_full_done, 1)
            for k in range(KH):
                for o in range(KH):
                    mm = pe.matmul(bank_m[k][:], cond[:, o, k * P:(k + 1) * P], wcat[:, o, 0:H],
                                   start=(o == 0), stop=(o == KH - 1))
                mm.then_inc(fold_ps, 1)
                for o in range(KH):
                    mm = pe.matmul(bank_ms[:, k * ZL:(k + 1) * ZL], cond[:, o, k * P:(k + 1) * P],
                                   wcat[:, o, H:MC], start=(o == 0), stop=(o == KH - 1))
                if k == KH - 1:
                    mm.then_inc(folds_ps, 1)
                if k == 1:
                    conv()
                if k == 2:
                    pe.wait_ge(wtot_read, 2)
                    weight_total(2, bank_total[2], len(DOWN_PARTS))

            x_transposes(0)

            def gate_up(b, c):
                n = chunk_no(b, c)
                f0, w = CHUNKS[c]
                if c == 0:
                    pe.wait_ge(xt_done, b + 1)
                if b == 0:
                    pe.wait_ge(tern_out, NC + c + 1)
                if n == 0:
                    pe.wait_ge(wtot_read, 3)
                if n == 1:
                    pe.wait_ge(ml_done, 2)
                if n >= 2:
                    pe.wait_ge(silu_done, n - 1)
                    pe.wait_ge(hmul_done, n - 1)
                for dst, w_t in ((bank_g[n % 2], tern_g), (bank_u[n % 2], tern_u)):
                    for k in range(KH):
                        mm = pe.matmul(dst[:, 0:w], xq_t[:, b % 2, k, :], w_t[:, k, f0:f0 + w],
                                       start=(k == 0), stop=(k == KH - 1))
                mm.then_inc(gu_ps, 1)

            def hidden_transposes(b):
                pe.wait_ge(hb_done, b + 1)
                for half, (j0, j1) in enumerate(((0, 6), (6, KF))):
                    if b == 0:
                        pe.wait_ge(ml_done, KH + 1)
                    else:
                        pe.wait_ge(ht_done, 3 * (b - 1) + 1 + 2 * half)
                    for j in range(j0, j1):
                        rows = P if j < KF - 1 else FL
                        mm = pe.transpose(bank_hT[half][0:rows, (j - j0) * P:(j - j0 + 1) * P],
                                          h_b[:, b % 2, j * P:j * P + rows], ident_b[:])
                    mm.then_inc(ht_ps, 1)

            def down(b):
                if b == 0:
                    pe.wait_ge(tern_out, 2 * NC + len(DOWN_PARTS))
                else:
                    pe.wait_ge(x1l_done, b)
                pe.wait_ge(ht_done, 3 * (b + 1))
                for j in range(KF):
                    rows = P if j < KF - 1 else FL
                    mm = pe.matmul(bank_down[:], h_t[0:rows, b % 2, j, :], tern_d[0:rows, j, :],
                                   start=(j == 0), stop=(j == KF - 1))
                mm.then_inc(down_ps, 1)

            def x1_transposes(b):
                pe.wait_ge(x1_done, b + 1)
                for k in range(KH):
                    mm = pe.transpose(bank_down[:, k * P:(k + 1) * P], xs[:, b, k * P:(k + 1) * P], ident[:])
                mm.then_inc(x1t_ps, 1)

            def z_logits(half):
                b0 = 4 * half
                pe.wait_ge(x1l_done, b0 + 4)
                if half == 0:
                    pe.wait_ge(xt_done, NB)
                else:
                    pe.wait_ge(ht_done, 3 * NB)
                n = 0
                for k in range(KH):
                    for m, a in ((m_h, x1t_h), (m_h, x1t_l), (m_l, x1t_h)):
                        mm = pe.matmul(bank_zt[half][0:ZL, :], m[:, k, H:MC], a[:, b0:b0 + 4, k, :],
                                       start=(n == 0), stop=(n == 3 * KH - 1))
                        n += 1
                mm.then_inc(zlt_ps, 1)

            def z_rows():
                pe.wait_ge(zlt_done, 2)
                for b in range(NB):
                    mm = pe.transpose(bank_zr[:, b * ZL:(b + 1) * ZL], zlt[:, b * P:(b + 1) * P],
                                      ident[0:ZL, 0:ZL])
                mm.then_inc(zl_ps, 1)

            def layer1(b):
                if b < 4:
                    n = chunk_no(NB - 1, NC - 1) - (1 if b // 2 != (NC * NB - 1) % 2 else 0)
                    pe.wait_ge(silu_done, n + 1)
                    pe.wait_ge(hmul_done, n + 1)
                elif b == 4:
                    pe.wait_ge(x1l_done, NB)
                elif b == 5:
                    pe.wait_ge(zs_done, 1)
                else:
                    pe.wait_ge(res_done, b - 5)
                pe.wait_ge(x1l_done, b + 1)
                n = 0
                for k in range(KH):
                    for a, m in ((x1t_h, m_h), (x1t_h, m_l), (x1t_l, m_h)):
                        pe.matmul(bank_y[b][:], a[:, b, k, :], m[:, k, 0:H], start=(n == 0), stop=False)
                        n += 1

            def experts(b):
                pe.wait_ge(zt_done, b // 4 + 1)
                pe.wait_ge(b_done, 1)
                pe.matmul(bank_y[b][:], zt[:, b, :], b_stack[:], start=False, stop=True).then_inc(y_ps, 1)

            for b in range(NB):
                gate_up(b, 0)
                if b >= 2:
                    x1_transposes(b - 2)
                gate_up(b, 1)
                if b >= 1:
                    hidden_transposes(b - 1)
                if b + 1 < NB:
                    x_transposes(b + 1)
                gate_up(b, 2)
                if b >= 1:
                    down(b - 1)
            last = NB - 1
            layer1(0)
            x1_transposes(last - 1)
            hidden_transposes(last)
            layer1(1)
            down(last)
            layer1(2)
            x1_transposes(last)
            z_logits(0)
            z_logits(1)
            layer1(3)
            z_rows()
            layer1(4)
            pe.wait_ge(zs_done, 1)
            for b in range(NB):
                mm = pe.transpose(bank_zs[b // 4][0:ZS, (b % 4) * P:(b % 4 + 1) * P], zstack[:, b, :], ident[:])
                if b % 4 == 3:
                    mm.then_inc(zt_ps, 1)
            for b in range(NB):
                if b >= 5:
                    layer1(b)
                experts(b)

        @block.vector
        def _(dve):
            links = [0]

            def link(ins):
                links[0] += 1
                ins.then_inc(dve_chain, 1)
                dve.wait_ge(dve_chain, links[0])

            dve.memset(wsum[:], 0.0).then_inc(eps_done, 1)
            link(dve.memset(eps12[:], 1e-12))
            dve.wait_ge(iota_done, 1)
            dve.tensor_scalar(ident[:], diff[:], 0.0, None, ALU.is_equal).then_inc(ident_done, 1)
            dve.tensor_scalar(ident_b[:], diff[:], 0.0, None, ALU.is_equal).then_inc(ident_done, 1)

            dve.wait_ge(ld_small, 16)
            link(dve.tensor_reduce(cbm[:, 0:1], cb, AX.X, ALU.max, apply_absolute_value=True))
            link(dve.tensor_scalar(cbm[:, 1:2], cbm[:, 0:1], 1e-8, None, ALU.max))
            link(dve.reciprocal(cbm[:, 2:3], cbm[:, 1:2]))
            link(dve.tensor_scalar(cbn[:], cb, cbm[:, 2:3], None, ALU.mult))
            link(dve.tensor_tensor(th[:], cbn[:, 0:NT], cbn[:, 1:NCB], ALU.add))
            dve.tensor_tensor(step[:], cbn[:, 1:NCB], cbn[:, 0:NT], ALU.subtract)
            link(dve.tensor_scalar(th[:], th[:], 0.5, None, ALU.mult))
            def t(i):
                return th[:, i:i + 1]
            link(dve.tensor_copy(step_h[:], step[:]))
            dve.tensor_tensor(step_l[:], step[:], step_h[:].bitcast(F32), ALU.subtract).then_inc(step_done, 1)
            dve.tensor_tensor(t(1), t(1), t(3), ALU.min)
            link(dve.tensor_tensor(t(5), t(5), t(3), ALU.max))
            dve.tensor_tensor(t(0), t(0), t(1), ALU.min)
            dve.tensor_tensor(t(6), t(6), t(5), ALU.max)
            dve.tensor_scalar(t(2), t(2), t(1), t(3), ALU.max, ALU.min)
            link(dve.tensor_scalar(t(4), t(4), t(3), t(5), ALU.max, ALU.min))
            link(dve.tensor_copy(act_f[:], act_i))
            dve.tensor_scalar(act_n[:], act_f[:], 0.0, float(NE), ALU.is_lt, ALU.mult)
            link(dve.tensor_copy(len_f[:], len_i))
            link(dve.tensor_tensor(act_f[:], act_f[:], act_n[:], ALU.add))
            link(dve.tensor_scalar(act_f[:], act_f[:], 0.0, float(NE - 1), ALU.max, ALU.min))
            dve.reciprocal(len_r[:], len_f[:])
            link(dve.tensor_scalar(act8[:], act_f[:], float(RK), None, ALU.mult))
            dve.wait_ge(iota_done, 4)
            act8_rep = act8[:].unsqueeze(2).broadcast_to([P, NACT, RK])
            for i in range(3):
                dve.tensor_tensor(sel_er[:, i * ZC:(i + 1) * ZC].rearrange("p (a r) -> p a r", a=NACT),
                                  pick[:], act8_rep, ALU.is_equal)
            dve.tensor_tensor(sel_e[:], part[0:NE, 0:1].broadcast_to([NE, NACT]), act_f[0:NE, :],
                              ALU.is_equal).then_inc(sel_done, 1)

            dve.wait_ge(scl_done, 1)
            link(dve.reciprocal(scl_inv[:], scl[:]))
            for k in range(KH):
                dve.wait_ge(delta_ps, k + 1)
                dve.wait_ge(ld_cond[k], 16)
                dve.tensor_tensor(cond[:, k, :], bank_delta[k][:], cond[:, k, :], ALU.add).then_inc(norm_step, 1)
                if k % 2 == 1:
                    dve.wait_ge(norm_step, k + 1)
                    v = cond[:, k, :].rearrange("p (g i) -> p g i", g=KH)
                    dve.tensor_tensor(v, v, scl_inv[:, k, :].unsqueeze(2).broadcast_to([P, KH, GROUP]),
                                      ALU.mult).then_inc(norm_done, 1)
                if k == 1:
                    dve.wait_ge(ld_exp, 48)
                    dve.tensor_copy(pr_bc[:], pr.unsqueeze(2).broadcast_to([NE, 2, P])).then_inc(sel_done, 1)
            dve.wait_ge(norm_done, KH)

            def x_sum(b):
                dve.wait_ge(ld_x[b], 16)
                link(dve.scalar_tensor_tensor(junk[:], t_iota[:], len_f[:, b:b + 1], xs[:, b, :], ALU.is_lt,
                                              ALU.mult, accum_out=ysum[:, b:b + 1]))

            for i in range(NT):
                if i >= 4:
                    dve.wait_ge(mask_used, i - 3)
                dve.tensor_scalar(mask[i % 4], cond[:], t(i), None, ALU.is_gt).then_inc(mask_done, 1)
                if i == 3:
                    x_sum(0)
                    x_sum(1)
            def weight_scale(i, src):
                dve.wait_ge(wtot_ps, i + 1)
                dve.tensor_reduce(wtot[:, i:i + 1], src, AX.X, ALU.add).then_inc(wtot_read, 1)
                dve.wait_ge(wtot_read, i + 1)
                link(dve.tensor_scalar(wscale[:, i:i + 1], wtot[:, i:i + 1], 1.0 / NW, EPS, ALU.mult, ALU.max))
                dve.tensor_scalar(w127[:, i:i + 1], wscale[:, i:i + 1], 1.0 / QMAX, None, ALU.mult)
                dve.reciprocal(winv[:, i:i + 1], wscale[:, i:i + 1]).then_inc(winv_done, 1)
                dve.wait_ge(winv_done, i + 1)

            def ternary(i, dst, src, n_before, buf, rows=P, rounded_by_act=0):
                n = src.shape[1] * src.shape[2]
                tmp = tern_i[0:rows, buf, 0:n].rearrange("p (k f) -> p k f", k=src.shape[1])
                if rounded_by_act:
                    dve.wait_ge(tern_int, rounded_by_act)
                else:
                    if n_before >= 1:
                        dve.wait_ge(tern_out, n_before)
                    link(dve.tensor_scalar(tmp, src, winv[0:rows, i:i + 1], None, ALU.mult))
                dve.tensor_scalar(dst, tmp, 1.0, -1.0, ALU.min, ALU.max).then_inc(tern_out, 1)

            def ternary_gate(c):
                f0, w = CHUNKS[c]
                ternary(0, tern_g[:, :, f0:f0 + w], raw_gate[:, :, f0:f0 + w], c, c % 2)

            x_sum(2)
            x_sum(3)
            weight_scale(0, bank_total[0])
            ternary_gate(0)

            for k in range(KH):
                dve.wait_ge(cb_ps, k + 1)
                v = cond[:, k, :].rearrange("p (g i) -> p g i", g=KH)
                dve.scalar_tensor_tensor(v, bank_cb[k][:].rearrange("p (g i) -> p g i", g=KH), cbn[:, 0:1],
                                         scl[:, k, :].unsqueeze(2).broadcast_to([P, KH, GROUP]),
                                         ALU.add, ALU.mult).then_inc(value_done, 1)
            dve.wait_ge(delta_done, KH)
            dve.wait_ge(value_done, KH)
            for k in range(1, KH, 2):
                dve.tensor_tensor(cond[:, k, :], cond[:, k, :], delta[:, k, :], ALU.add).then_inc(weff_done, 1)
            ternary_gate(1)
            ternary_gate(2)
            dve.wait_ge(sel_ps, 1)
            sel_v = bank_sel[:, 0:KH * ZL].rearrange("p (k c) -> p k c", k=KH)
            dve.tensor_copy(wcat[:, :, H:MC], sel_v).then_inc(sel_read, 1)
            dve.tensor_copy(lg[:, 0:2, :], bank_sel[:, KH * ZL:KH * ZL + 2 * NACT]
                            .rearrange("p (i a) -> p i a", i=2)).then_inc(sel_read, 2)
            for b in range(4, NB):
                x_sum(b)
            dve.tensor_tensor(ymean[:], ysum[:], len_r[:], ALU.mult).then_inc(ymean_done, 1)
            weight_scale(1, bank_total[1])
            for c, (f0, w) in enumerate(CHUNKS):
                ternary(1, tern_u[:, :, f0:f0 + w], raw_up[:, :, f0:f0 + w], NC + c, c % 2,
                        rounded_by_act=1 if c == UP_ROUNDED_BY_ACT else 0)

            link(dve.tensor_reduce(rmax[:], xs[:], AX.X, ALU.max, apply_absolute_value=True))
            dve.wait_ge(yexp_done, 1)
            link(dve.tensor_scalar(yexp[:], yexp[:], 1.0, None, ALU.add))
            link(dve.reciprocal(gate[:], yexp[:]))
            link(dve.tensor_tensor(arow[:], rmax[:], gate[:], ALU.mult))
            link(dve.tensor_scalar(arow[:], arow[:], EPS, None, ALU.max))
            link(dve.reciprocal(qx[:], arow[:]))
            dve.tensor_scalar(s_g[:], arow[:], w127[:, 0:1], None, ALU.mult)
            dve.tensor_scalar(s_u[:], arow[:], w127[:, 1:2], None, ALU.mult)
            link(dve.tensor_scalar(qx[:], qx[:], QMAX, None, ALU.mult))
            weight_scale(2, bank_total[2])

            def x_quantise(b):
                link(dve.tensor_scalar(xq_i[:, b % 2, :], xs[:, b, :], gate[:, b:b + 1], qx[:, b:b + 1],
                                       ALU.mult, ALU.mult))
                if b >= 2:
                    dve.wait_ge(xt_ps, b - 1)
                dve.tensor_copy(xq_b[:, b % 2, :], xq_i[:, b % 2, :]).then_inc(xq_done, 1)

            x_quantise(0)
            x_quantise(1)

            def stacked_b():
                dve.wait_ge(b_full_done, 1)
                dve.wait_ge(rows_done, 5)
                link(dve.tensor_copy(b_high, b_full[:]))
                link(dve.tensor_scalar(b_full[:], b_full[:], low_row[0:ZS, :], None, ALU.mult))
                dve.scalar_tensor_tensor(b_stack[:], b_high.bitcast(F32), sign_row[0:ZS, :], b_full[:],
                                         ALU.mult, ALU.add).then_inc(b_done, 1)
                dve.wait_ge(lp_done, 1)
                link(dve.tensor_tensor(log_prior[:], log_prior[:], lg[:, 1, :], ALU.add))

            def m_low(k):
                dve.wait_ge(mh_done, k + 1)
                if k < KH:
                    dst, src, high = m_l[:, k, 0:H], bank_m[k][:], m_h[:, k, 0:H]
                else:
                    src = bank_ms[:, 0:KH * ZL].rearrange("p (k c) -> p k c", k=KH)
                    dst, high = m_l[:, :, H:MC], m_h[:, :, H:MC]
                dve.tensor_tensor(dst, src, high.bitcast(F32), ALU.subtract).then_inc(ml_done, 1)

            m_low(0)
            m_low(1)
            for i, (j0, n, rows) in enumerate(DOWN_PARTS):
                ternary(2, tern_d[0:rows, j0:j0 + n, :], raw_down[0:rows, j0:j0 + n, :], 2 * NC + i, i % 2,
                        rows, rounded_by_act=2 + i // 2 if i % 2 == 0 else 0)

            def hidden_chunk(b, c):
                n = chunk_no(b, c)
                f0, w = CHUNKS[c]
                dve.wait_ge(silu_done, n + 1)
                if c == 0 and b >= 2:
                    dve.wait_ge(hint_done, b - 1)
                if n == 0:
                    dve.wait_ge(tern_out, 2 * NC)
                hs = hbuf[b % 2][:, f0:f0 + w]
                dve.tensor_tensor(hs, bank_u[n % 2][:, 0:w], silu[:, n % 2, 0:w], ALU.mult)\
                    .then_inc(hmul_done, 1)
                dve.wait_ge(hmul_done, n + 1)
                link(dve.tensor_reduce(hmax[:, b % 2, c:c + 1], hs, AX.X, ALU.max, apply_absolute_value=True))

            def hidden_scale(b):
                o = slice(b, b + 1)
                link(dve.tensor_reduce(hred[:, o], hmax[:, b % 2, :], AX.X, ALU.max))
                link(dve.tensor_scalar(harow[:, o], hred[:, o], s_u[:, o], EPS, ALU.mult, ALU.max))
                link(dve.reciprocal(hrec[:, o], harow[:, o]))
                dve.tensor_scalar(hq[:, o], hrec[:, o], QMAX, s_u[:, o], ALU.mult, ALU.mult)\
                    .then_inc(hscale_done, 1)

            def hidden_bf16(b):
                dve.wait_ge(hint_done, b + 1)
                if b >= 2:
                    dve.wait_ge(ht_ps, 2 * (b - 1))
                dve.tensor_copy(h_b[:, b % 2, :], h_i[:, b % 2, :]).then_inc(hb_done, 1)

            def residual(b):
                o = slice(b, b + 1)
                link(dve.tensor_scalar(s_d[:, o], harow[:, o], w127[:, 2:3], None, ALU.mult))
                dve.wait_ge(down_ps, b + 1)
                dve.scalar_tensor_tensor(xs[:, b, :], bank_down[:], s_d[:, o], xs[:, b, :],
                                         ALU.mult, ALU.add).then_inc(x1_done, 1)

            def x1_low(b):
                dve.wait_ge(x1h_done, b + 1)
                dve.tensor_tensor(x1t_l[:, b, :, :], bank_down[:].rearrange("p (k e) -> p k e", k=KH),
                                  x1t_h[:, b, :, :].bitcast(F32), ALU.subtract).then_inc(x1l_done, 1)

            stacked_b()
            for b in range(NB + 2):
                if 1 <= b <= NB:
                    hidden_bf16(b - 1)
                if b < NB:
                    hidden_chunk(b, 0)
                if b == 0:
                    for k in range(2, KH + 1):
                        m_low(k)
                if b >= 2:
                    x1_low(b - 2)
                if b < NB:
                    hidden_chunk(b, 1)
                if b + 2 < NB:
                    x_quantise(b + 2)
                if b < NB:
                    hidden_chunk(b, 2)
                    hidden_scale(b)
                if 1 <= b <= NB:
                    residual(b - 1)

            dve.wait_ge(zl_ps, 1)
            link(dve.tensor_copy(zl[:], bank_zr[:, 0:NB * ZL].rearrange("p (b c) -> p b c", b=NB)))
            link(dve.tensor_tensor(lg[:], zl[:, :, ZC:ZL], log_prior[:].unsqueeze(1).broadcast_to([P, NB, NACT]),
                                   ALU.add))
            link(dve.tensor_reduce(lmax[:], lg[:], AX.X, ALU.max))
            dve.tensor_tensor(lg[:], lg[:], lmax[:].unsqueeze(2).broadcast_to([P, NB, NACT]),
                              ALU.subtract).then_inc(lmax_done, 1)
            dve.wait_ge(ex_done, 1)
            link(dve.tensor_reduce(esum[:], ex[:], AX.X, ALU.add))
            link(dve.reciprocal(esum[:], esum[:]))
            link(dve.tensor_tensor(alpha[:], ex[:], esum[:].unsqueeze(2).broadcast_to([P, NB, NACT]), ALU.mult))
            for a in range(NACT):
                ins = dve.tensor_tensor(zz[:, :, a * RK:(a + 1) * RK], zl[:, :, a * RK:(a + 1) * RK],
                                        alpha[:, :, a:a + 1].broadcast_to([P, NB, RK]), ALU.mult)
            link(ins)
            link(dve.tensor_copy(zz_h[:], zz[:]))
            dve.memset(zstack[:, :, 3 * ZC:ZS], 1.0)
            high = zz_h[:].bitcast(F32)
            dve.tensor_copy(zstack[:, :, 0:ZC], high)
            dve.tensor_copy(zstack[:, :, 2 * ZC:3 * ZC], high)
            dve.tensor_tensor(zstack[:, :, ZC:2 * ZC], zz[:], high, ALU.subtract).then_inc(zs_done, 1)
            for b in range(NB):
                dve.wait_ge(y_ps, b + 1)
                dve.tensor_tensor(xs[:, b, :], bank_y[b][:], xs[:, b, :], ALU.add).then_inc(res_done, 1)


def kernel(x, itok_B_9_3973, condB_codebook, L0_cond_conv_w, L0_ffn_w_gate, L0_ffn_w_up, L0_ffn_w_down,
           L1_cond_weight, L1_cond_scale_log, L1_cond_lora_A, L1_cond_lora_B, L1_ffn_W_base, L1_ffn_b_base,
           L1_ffn_lora_A, L1_ffn_lora_B, L1_ffn_router_W, L1_ffn_router_b, L1_ffn_domain_prior, L1_ffn_active):
    import numpy as np
    import concourse.bacc as bacc
    from concourse.bass_utils import run_bass_kernel_spmd

    n = np.asarray
    layout = {
        "x": n(x),
        "small": np.concatenate([n(condB_codebook), n(L0_cond_conv_w).reshape(TAPS),
                                 n(itok_B_9_3973).view(np.float32), n(L1_ffn_active).view(np.float32)]),
        "w_gate_t": n(L0_ffn_w_gate).T,
        "w_up_t": n(L0_ffn_w_up).T,
        "w_down_t": n(L0_ffn_w_down).T,
        "cond_w": n(L1_cond_weight),
        "scale_log": n(L1_cond_scale_log).reshape(KH, P, KH).transpose(1, 0, 2),
        "lora0": np.stack([n(L1_cond_lora_A), n(L1_cond_lora_B).T], axis=1),
        "w_base_t": n(L1_ffn_W_base).T,
        "b_base": n(L1_ffn_b_base).reshape(1, H),
        "lora1": np.stack([n(L1_ffn_lora_A).reshape(NE * RK, H),
                           n(L1_ffn_lora_B).transpose(0, 2, 1).reshape(NE * RK, H)], axis=1),
        "router": np.concatenate([n(L1_ffn_router_W), n(L1_ffn_domain_prior).reshape(NE, 1),
                                  n(L1_ffn_router_b).reshape(NE, 1)], axis=1),
    }
    nc = bacc.Bacc("TRN2", target_bir_lowering=False, num_devices=1)
    arrays, args = {}, {}
    for name, a in layout.items():
        a = np.ascontiguousarray(a)
        arrays[f"in_{name}"] = a
        args[name] = nc.dram_tensor(f"in_{name}", a.shape, mybir.dt.from_np(a.dtype), kind="ExternalInput").ap()
    args["out"] = nc.dram_tensor("out_x", (NB, E, H), F32, kind="ExternalOutput").ap()
    build(nc, **args)
    r = run_bass_kernel_spmd(nc, [arrays], core_ids=[0])
    return r.results[0]["out_x"]
```

```python
from contextlib import ExitStack

import concourse.bass as bass
from concourse import mybir

F32 = mybir.dt.float32
F32R = mybir.dt.float32r
BF16 = mybir.dt.bfloat16
I16 = mybir.dt.int16
I32 = mybir.dt.int32
ALU = mybir.AluOpType
ACT = mybir.ActivationFunctionType
AX = mybir.AxisListType

P = 128
NB, E, H = 8, 128, 512
F = 1376
KH = H // P
KF = -(-F // P)
FL = F - (KF - 1) * P
CHUNKS = [(0, 464), (464, 464), (928, 448)]
NC = len(CHUNKS)
NCB = 8
NT = NCB - 1
GROUP = 128
RANK0 = 64
LORA0_FACTOR = 32.0 / RANK0
NE, NACT, RK = 16, 4, 8
ZC = NACT * RK
ZL = ZC + NACT
ZS = 3 * ZC + 2
TAPS = 5
SMALL = NCB + TAPS + NB + NACT
NW = float(F * H)
QMAX = 127.0
EPS = 1e-5
ROUND = 1.5 * 2 ** 23
WARM_UP = 3
ROW_BLOCKS = (0, 2, 1, 3)
DOWN_PARTS = [(0, 3, P), (3, 3, P), (6, 2, P), (8, 2, P), (KF - 1, 1, FL)]
RESULTS = [(b, 0, H) for b in range(NB - 1)] + [(NB - 1, 0, H // 2), (NB - 1, H // 2, H)]
DOWN_BY_ACT = (0, 2, 3, 4)


def build(nc, x, small, w_gate_t, w_up_t, w_down_t, cond_w, scale_log, lora0, w_base_t, b_base,
          lora1, router, out):
    with ExitStack() as ctx:
        def sb(name, shape, dt=F32):
            return ctx.enter_context(nc.sbuf_tensor(name, shape, dt))

        def sem(name):
            return ctx.enter_context(nc.semaphore(name))

        bank = [ctx.enter_context(nc.psum_tensor(f"bank{i}", [P, 512], F32)) for i in range(8)]
        bank_hT = [bank[0][:].bitcast(BF16), bank[1][:].bitcast(BF16)]
        bank_down = bank[2]
        bank_xT = bank[3][:].bitcast(BF16)
        bank_zt = [bank[3], bank[1]]
        bank_zr = bank[3]
        bank_zs = [bank[3], bank[1]]
        bank_m = [bank[7], bank[6], bank[0], bank[1]]
        bank_ms = bank[2]
        bank_delta = bank[0:4]
        bank_cb = bank[4:8]
        bank_sel = bank[0]
        bank_b = bank[1]
        bank_conv = bank[2][:, 0:NB]
        bank_total = [bank[3][:, 0:KH], bank[5][:, 0:KH], bank[1][:, 0:len(DOWN_PARTS)]]
        bank_warm = bank[4]
        bank_g = [bank[4], bank[6]]
        bank_u = [bank[5], bank[7]]
        bank_y = [bank[i] for i in (4, 5, 6, 7, 2, 0, 4, 5, 6)]

        xs = sb("xs", [P, NB, H])
        raw = [sb("raw_gate_down", [P, KF * H]), sb("raw_up", [P, KH * F])]
        raw_gate = raw[0][:, 0:KH * F].rearrange("p (k f) -> p k f", k=KH)
        raw_up = raw[1][:, :].rearrange("p (k f) -> p k f", k=KH)
        raw_down = raw[0][:, :].rearrange("p (j h) -> p j h", j=KF)
        cond = sb("cond", [P, KH, H])
        wbt = sb("wbt", [P, KH, H])
        lora_sb = sb("lora_sb", [P, 2, H])
        lora_a, lora_bt = lora_sb[0:RANK0, 0, :], lora_sb[0:RANK0, 1, :]
        slog = sb("slog", [P, KH, KH])
        small_sb = sb("small_sb", [P, SMALL])
        cb = small_sb[:, 0:NCB]
        cw = small_sb[:, NCB:NCB + TAPS]
        len_i = small_sb[:, NCB + TAPS:NCB + TAPS + NB].bitcast(I32)
        act_i = small_sb[:, NCB + TAPS + NB:SMALL].bitcast(I32)
        l1ab = sb("l1ab", [NE * RK, 2, H])
        l1a, l1b = l1ab[:, 0, :], l1ab[:, 1, :]
        rwp = sb("rwp", [NE, H + 2])
        rw, pr = rwp[:, 0:H], rwp[:, H:H + 2]
        bb = sb("bb", [1, H])

        t_iota = sb("t_iota", [P, H])
        diff = sb("diff", [P, P])
        pick = sb("pick", [P, NACT, RK])
        part = sb("part", [P, 1])
        ident = sb("ident", [P, P])
        ident_b = sb("ident_b", [P, P], BF16)
        fold_two = sb("fold_two", [P, ZL])
        fold_tmp = sb("fold_tmp", [P, ZL])
        ones = sb("ones", [P, P])
        bias_rows = sb("bias_rows", [1, ZS])
        low_row = sb("low_row", [P, 1])
        sign_row = sb("sign_row", [P, 1])
        tmp_row = sb("tmp_row", [P, 1])
        two_row = sb("two_row", [P, 1])

        cbm = sb("cbm", [P, 4])
        cbn = sb("cbn", [P, NCB])
        th = sb("th", [P, NT])
        step = sb("step", [P, NT])
        step_h = sb("step_h", [P, NT], F32R)
        step_l = sb("step_l", [P, NT])
        diag_h = sb("diag_h", [P, NB, P], F32R)
        diag_l = sb("diag_l", [P, NT, P], F32R)
        scl = sb("scl", [P, KH, KH])
        scl_inv = sb("scl_inv", [P, KH, KH])
        delta = sb("delta", [P, KH, H])
        fr = sb("fr", [P, 4, KH * H], F32R)
        mask = [fr[:, i, :].rearrange("p (k h) -> p k h", k=KH) for i in range(4)]
        x1t_h = fr[:, 0:2, :].rearrange("p a (b k e) -> p (a b) k e", b=4, k=KH)
        x1t_l = fr[:, 2:4, :].rearrange("p a (b k e) -> p (a b) k e", b=4, k=KH)

        table_use = sb("table_use", [P, 1])
        junk = sb("junk", [P, H])
        act_f = sb("act_f", [P, NACT])
        act_n = sb("act_n", [P, NACT])
        act8 = sb("act8", [P, NACT])
        sel_er = sb("sel_er", [P, ZS])
        sel_e = sb("sel_e", [NE, NACT])
        pr_bc = sb("pr_bc", [NE, 2, P])
        log_prior = sb("log_prior", [P, NACT])
        eps12 = sb("eps12", [P, 1])
        b_full = sb("b_full", [ZS, H])
        b_high = fr[0:ZS, 3, 3 * H:4 * H]
        b_stack = sb("b_stack", [ZS, H], F32R)

        len_f = sb("len_f", [P, NB])
        len_r = sb("len_r", [P, NB])
        ysum = sb("ysum", [P, NB])
        ymean = sb("ymean", [P, NB])
        band = sb("band", [P, P])
        band_t = sb("band_t", [P, P])
        yexp = sb("yexp", [P, NB])
        gate = sb("gate", [P, NB])
        rmax = sb("rmax", [P, NB])
        arow = sb("arow", [P, NB])
        qx = sb("qx", [P, NB])
        s_g = sb("s_g", [P, NB])
        s_u = sb("s_u", [P, NB])
        wsum = sb("wsum", [P, 3, len(DOWN_PARTS)])
        wtot = sb("wtot", [P, 3])
        wscale = sb("wscale", [P, 3])
        winv = sb("winv", [P, 3])
        w127 = sb("w127", [P, 3])
        tern_g = sb("tern_g", [P, KH, F], BF16)
        tern_u = sb("tern_u", [P, KH, F], BF16)
        tern_d = sb("tern_d", [P, KF, H], BF16)
        junk_a = tern_d[:].rearrange("p j h -> p (j h)")[:, 0:4 * H]
        tern_i = sb("tern_i", [P, 2, KH * CHUNKS[0][1]], I16)
        xq_i = lora_sb[:, 0, :].bitcast(I16).rearrange("p (i h) -> p i h", i=2)
        xq_b = lora_sb[:, 1, :].bitcast(BF16).rearrange("p (i h) -> p i h", i=2)
        xq_t = l1a.bitcast(BF16).rearrange("p (i k e) -> p i k e", i=2, k=KH)
        cond_flat = cond[:].rearrange("p k h -> p (k h)")
        silu = cond_flat[:, 0:2 * CHUNKS[0][1]].rearrange("p (i f) -> p i f", i=2)
        hbuf = [raw[1][:, i * F:(i + 1) * F] for i in range(2)]
        h_i = raw[1][:, 2 * F:3 * F].bitcast(I16).rearrange("p (i f) -> p i f", i=2)
        h_b = raw[1][:, 3 * F:4 * F].bitcast(BF16).rearrange("p (i f) -> p i f", i=2)
        hmax = sb("hmax", [P, 2, NC])
        hred = sb("hred", [P, NB])
        harow = sb("harow", [P, NB])
        hrec = sb("hrec", [P, NB])
        hq = sb("hq", [P, NB])
        s_d = sb("s_d", [P, NB])
        h_t = delta[:].rearrange("p k h -> p (k h)")[:, 0:KF * P].bitcast(BF16)\
            .rearrange("p (i j e) -> p i j e", i=2, j=KF)

        ms_t = delta[0:2 * ZL, 0, :]
        m_h = sb("m_h", [P, KH, H], F32R)
        m_l = sb("m_l", [P, KH, H], F32R)
        m_s = sb("m_s", [P, KH, 2 * ZL], F32R)
        ms_h, ms_l = m_s[:, :, 0:ZL], m_s[:, :, ZL:2 * ZL]
        w_h, w_l = mask[0], mask[1]
        m_full = wbt
        wbt_flat = wbt[:].rearrange("p k c -> p (k c)")
        zstack = wbt_flat[:, 0:NB * ZS].rearrange("p (b c) -> p b c", b=NB)
        zlt = raw[1][0:2 * ZL, 0:NB * P]
        zl = wbt_flat[:, NB * ZS:NB * (ZS + ZL)].rearrange("p (b c) -> p b c", b=NB)
        zz = wbt_flat[:, NB * (ZS + ZL):NB * (ZS + ZL + ZC)].rearrange("p (b c) -> p b c", b=NB)
        lg = sb("lg", [P, NB, NACT])
        lmax = sb("lmax", [P, NB])
        ex = sb("ex", [P, NB, NACT])
        esum = sb("esum", [P, NB])
        alpha = sb("alpha", [P, NB, NACT])
        zz_h = diag_l[:].rearrange("p t c -> p (t c)")[:, 0:NB * ZC].rearrange("p (b c) -> p b c", b=NB)
        zt = diag_h[0:ZS, :, :]

        ld_small, ld_lora, ld_slog, ld_exp = sem("ld_small"), sem("ld_lora"), sem("ld_slog"), sem("ld_exp")
        ld_cond = [sem(f"ld_cond{k}") for k in range(KH)]
        ld_wbase = sem("ld_wbase")
        ld_x = [sem(f"ld_x{b}") for b in range(NB)]
        ld_gate = [sem(f"ld_gate{k}") for k in range(KH)]
        ld_up = [sem(f"ld_up{k}") for k in range(KH)]
        ld_down = [sem(f"ld_down{i}") for i in range(len(DOWN_PARTS))]
        stored = sem("stored")
        iota_done = sem("iota_done")
        ident_done = sem("ident_done")
        eps_done = sem("eps_done")
        lora_scaled = sem("lora_scaled")
        delta_ps = sem("delta_ps")
        norm_step = sem("norm_step")
        norm_done = sem("norm_done")
        step_done = sem("step_done")
        b_full_done = sem("b_full_done")
        rows_done = sem("rows_done")
        delta_done = sem("delta_done")
        scl_done = sem("scl_done")
        diag_done = sem("diag_done")
        sel_done = sem("sel_done")
        sel_ps = sem("sel_ps")
        sel_read = sem("sel_read")
        b_ps = sem("b_ps")
        b_done = sem("b_done")
        lp_done = sem("lp_done")
        mask_done = sem("mask_done")
        mask_used = sem("mask_used")
        cb_ps = sem("cb_ps")
        value_done = sem("value_done")
        weff_even = sem("weff_even")
        weff_odd = sem("weff_odd")
        wh_done = sem("wh_done")
        wl_even = sem("wl_even")
        wl_odd = sem("wl_odd")
        ch_done = sem("ch_done")
        cl_done = sem("cl_done")
        qx_done = sem("qx_done")
        xf_done = sem("xf_done")
        band_done = sem("band_done")
        band_step = sem("band_step")
        ymean_done = sem("ymean_done")
        conv_ps = sem("conv_ps")
        yexp_done = sem("yexp_done")
        wsum_done = [sem("gsum_done"), sem("usum_done"), sem("dsum_done")]
        wtot_ps = sem("wtot_ps")
        wtot_read = sem("wtot_read")
        winv_done = sem("winv_done")
        tern_int = sem("tern_int")
        tern_out = sem("tern_out")
        fold_ps = sem("fold_ps")
        mst_ps = sem("mst_ps")
        mst_done = sem("mst_done")
        folds_ps = sem("folds_ps")
        msh_done = sem("msh_done")
        msl_done = sem("msl_done")
        m_out = sem("m_out")
        mh_done = sem("mh_done")
        ml_done = sem("ml_done")
        xq_done = sem("xq_done")
        xt_ps = sem("xt_ps")
        xt_done = sem("xt_done")
        gu_ps = sem("gu_ps")
        silu_done = sem("silu_done")
        hmul_done = sem("hmul_done")
        hscale_done = sem("hscale_done")
        hint_done = sem("hint_done")
        hb_done = sem("hb_done")
        ht_ps = sem("ht_ps")
        ht_done = sem("ht_done")
        down_ps = sem("down_ps")
        x1_done = sem("x1_done")
        x1t_ps = sem("x1t_ps")
        x1h_done = sem("x1h_done")
        x1l_done = sem("x1l_done")
        zlt_ps = sem("zlt_ps")
        zlt_done = sem("zlt_done")
        zl_ps = sem("zl_ps")
        lmax_done = sem("lmax_done")
        ex_done = sem("ex_done")
        zs_done = sem("zs_done")
        zt_ps = sem("zt_ps")
        zt_done = sem("zt_done")
        y_ps = sem("y_ps")
        res_done = sem("res_done")
        dve_chain = sem("dve_chain")

        def chunk_no(b, c):
            return NC * b + c

        block = ctx.enter_context(nc.Block())

        @block.sync
        def _(sp):
            cond_v = cond_w.rearrange("(k p) h -> p k h", p=P)
            for k in range(KH):
                sp.dma_start(cond[:, k, :], cond_v[:, k, :]).then_inc(ld_cond[k], 16)
            sp.dma_start(l1ab[:], lora1).then_inc(ld_exp, 16)
            sp.dma_start(rwp[:], router).then_inc(ld_exp, 16)
            sp.dma_start(bb[:], b_base).then_inc(ld_exp, 16)
            sp.dma_start(wbt[:], w_base_t.rearrange("(k p) c -> p k c", p=P)).then_inc(ld_wbase, 16)
            for b in range(NB):
                sp.dma_start(xs[:, b, :], x[b]).then_inc(ld_x[b], 16)
            gate_v = w_gate_t.rearrange("(k p) f -> p k f", p=P)
            up_v = w_up_t.rearrange("(k p) f -> p k f", p=P)
            for k in range(KH):
                sp.dma_start(raw_gate[:, k, :], gate_v[:, k, :]).then_inc(ld_gate[k], 16)
            for k in range(KH):
                sp.dma_start(raw_up[:, k, :], up_v[:, k, :]).then_inc(ld_up[k], 16)
            sp.wait_ge(tern_out, NC)
            for i, (j0, n, rows) in enumerate(DOWN_PARTS):
                src = w_down_t[j0 * P:j0 * P + (n - 1) * P + rows, :].rearrange("(j p) h -> p j h", p=rows)
                sp.dma_start(raw_down[0:rows, j0:j0 + n, :], src).then_inc(ld_down[i], 16)
            for n, (b, h0, h1) in enumerate(RESULTS):
                sp.wait_ge(res_done, n + 1)
                sp.dma_start(out[b, :, h0:h1], xs[:, b, h0:h1]).then_inc(stored, 16)
            sp.wait_ge(stored, 16 * len(RESULTS))

        @block.gpsimd
        def _(pool):
            pool.iota(diff[:], [[-1, P]], 0, 1, allow_small_or_imprecise_dtypes=True).then_inc(iota_done, 1)
            pool.iota(pick[:], [[0, NACT], [-1, RK]], 0, 1, allow_small_or_imprecise_dtypes=True).then_inc(iota_done, 1)
            pool.iota(part[:], [[0, 1]], 0, 1, allow_small_or_imprecise_dtypes=True).then_inc(iota_done, 1)
            pool.memset(sel_er[:], 0.0).then_inc(iota_done, 1)
            pool.iota(t_iota[:], [[1, H]], 0, 0, allow_small_or_imprecise_dtypes=True).then_inc(iota_done, 1)
            pool.memset(ones[:], 1.0).then_inc(iota_done, 1)
            pool.memset(bias_rows[:], 1.0).then_inc(iota_done, 1)
            pool.wait_ge(iota_done, 7)
            pool.memset(bias_rows[:, 0:3 * ZC], 0.0).then_inc(iota_done, 2)

            pool.tensor_scalar(low_row[:], part[:], float(2 * ZC), None, ALU.is_ge).then_inc(rows_done, 1)
            pool.tensor_scalar(tmp_row[:], part[:], float(3 * ZC), None, ALU.is_equal).then_inc(rows_done, 1)
            pool.wait_ge(rows_done, 2)
            pool.tensor_tensor(low_row[:], low_row[:], tmp_row[:], ALU.subtract).then_inc(rows_done, 1)
            pool.wait_ge(rows_done, 3)
            pool.tensor_scalar(sign_row[:], low_row[:], -2.0, 1.0, ALU.mult, ALU.add).then_inc(rows_done, 1)
            pool.tensor_scalar(two_row[:], part[:], float(3 * ZC), 1.0, ALU.is_lt, ALU.add).then_inc(rows_done, 1)

            pool.tensor_scalar(fold_two[:], diff[:, 0:ZL], 0.0, None, ALU.is_equal).then_inc(rows_done, 1)
            pool.tensor_scalar(fold_tmp[:], diff[:, 0:ZL], float(ZL), None, ALU.is_equal).then_inc(rows_done, 1)
            pool.wait_ge(rows_done, 7)
            pool.tensor_tensor(fold_two[:], fold_two[:], fold_tmp[:], ALU.add).then_inc(rows_done, 1)

            for k in range(0, KH, 2):
                pool.wait_ge(norm_step, k + 1)
                v = cond[:, k, :].rearrange("p (g i) -> p g i", g=KH)
                pool.tensor_tensor(v, v, scl_inv[:, k, :].unsqueeze(2).broadcast_to([P, KH, GROUP]),
                                   ALU.mult).then_inc(norm_done, 1)

            pool.wait_ge(ld_small, 16)
            pool.tensor_scalar(band[:], diff[:], -2.0, cw[:, 0:1], ALU.is_equal, ALU.mult).then_inc(band_step, 1)
            for i in range(1, TAPS):
                pool.tensor_scalar(band_t[:], diff[:], float(i - 2), cw[:, i:i + 1], ALU.is_equal,
                                   ALU.mult).then_inc(band_step, 1)
                pool.wait_ge(band_step, 2 * i)
                pool.tensor_tensor(band[:], band[:], band_t[:], ALU.add)\
                    .then_inc(band_step if i < TAPS - 1 else band_done, 1)
                if i < TAPS - 1:
                    pool.wait_ge(band_step, 2 * i + 1)

            pool.wait_ge(ch_done, 1)
            pool.tensor_tensor(m_l[:], wbt[:], m_h[:].bitcast(F32), ALU.subtract)\
                .then_inc(cl_done, 1)

            pool.wait_ge(delta_done, KH)
            for k in range(0, KH, 2):
                pool.wait_ge(value_done, k + 1)
                pool.tensor_tensor(cond[:, k, :], cond[:, k, :], delta[:, k, :], ALU.add).then_inc(weff_even, 1)
            for k in range(0, KH, 2):
                pool.wait_ge(wh_done, ROW_BLOCKS.index(k) + 1)
                pool.tensor_tensor(w_l[:, k, :], cond[:, k, :], w_h[:, k, :].bitcast(F32),
                                   ALU.subtract).then_inc(wl_even, 1)

            pool.wait_ge(xq_done, 1)
            for b in range(1, NB):
                pool.wait_ge(qx_done, 1 + b // 2)
                if b >= 2:
                    pool.wait_ge(xq_done, b)
                pool.tensor_scalar(junk[:], xs[:, b, :], gate[:, b:b + 1], qx[:, b:b + 1],
                                   ALU.mult, ALU.mult).then_inc(xf_done, 1)
                pool.wait_ge(xf_done, b)
                if b >= 2:
                    pool.wait_ge(xt_ps, b - 1)
                pool.tensor_scalar(xq_b[:, b % 2, :], junk[:], ROUND, ROUND, ALU.add,
                                   ALU.subtract).then_inc(xq_done, 1)

            for k in range(KH):
                pool.wait_ge(mh_done, k + 1)
                pool.tensor_tensor(m_l[:, k, :], m_full[:, k, :], m_h[:, k, :].bitcast(F32),
                                   ALU.subtract).then_inc(ml_done, 1)

        @block.scalar
        def _(act):
            act.dma_start(small_sb[:], small.partition_broadcast(P)).then_inc(ld_small, 16)
            act.dma_start(lora_sb[0:RANK0, :, :], lora0).then_inc(ld_lora, 16)
            act.dma_start(slog[:], scale_log).then_inc(ld_slog, 16)

            act.wait_ge(iota_done, 3)
            act.activation(table_use[:], part[:], ACT.Exp, scale=0.0)
            act.wait_ge(ld_lora, 16)
            act.activation(lora_a, lora_a, ACT.Copy, scale=LORA0_FACTOR).then_inc(lora_scaled, 1)

            def diagonals(i):
                act.activation(diag_h[:, i, :], ident[:], ACT.Copy,
                               scale=step_h[:, i:i + 1].bitcast(F32)).then_inc(diag_done, 1)
                act.activation(diag_l[:, i, :], ident[:], ACT.Copy, scale=step_l[:, i:i + 1]).then_inc(diag_done, 1)

            act.wait_ge(ident_done, 2)
            act.wait_ge(step_done, 1)
            diagonals(0)
            act.wait_ge(ld_slog, 16)
            act.activation(scl[:], slog[:], ACT.Exp).then_inc(scl_done, 1)
            diagonals(1)
            for k in range(KH):
                act.wait_ge(norm_step, k + 1)
                act.activation(delta[:, k, :], bank_delta[k][:], ACT.Copy).then_inc(delta_done, 1)
            for i in range(2, NT):
                diagonals(i)

            act.wait_ge(ld_wbase, 16)
            act.activation(m_h[:], wbt[:], ACT.Copy).then_inc(ch_done, 1)

            def weight_sum(i, k, src, rows=P):
                n = src.shape[1] * (src.shape[2] if len(src.shape) > 2 else 1)
                dst = junk_a[0:rows, 0:n]
                if k > 0:
                    act.wait_ge(wsum_done[i], k)
                elif i > 0:
                    act.wait_ge(wsum_done[i - 1], KH)
                if len(src.shape) > 2:
                    dst = dst.rearrange("p (j h) -> p j h", j=src.shape[1])
                act.activation(dst, src, ACT.Abs, accum_out=wsum[0:rows, i, k:k + 1]).then_inc(wsum_done[i], 1)

            act.wait_ge(eps_done, 1)
            for k in range(KH):
                act.wait_ge(ld_gate[k], 16)
                weight_sum(0, k, raw_gate[:, k, :])

            def weight_sum_up(k):
                act.wait_ge(ld_up[k], 16)
                weight_sum(1, k, raw_up[:, k, :])

            def rounded_chunk(i, c):
                n = i * NC + c
                f0, w = CHUNKS[c]
                act.wait_ge(winv_done, i + 1)
                if n >= 2:
                    act.wait_ge(tern_out, n - 1)
                src = (raw_gate, raw_up)[i]
                act.activation(tern_i[:, n % 2, 0:KH * w].rearrange("p (k f) -> p k f", k=KH),
                               src[:, :, f0:f0 + w], ACT.Copy, scale=winv[:, i:i + 1]).then_inc(tern_int, 1)

            weight_sum_up(0)
            for n, k in enumerate(ROW_BLOCKS):
                act.wait_ge(*((weff_even, k // 2 + 1) if k % 2 == 0 else (weff_odd, k // 2 + 1)))
                act.activation(w_h[:, k, :], cond[:, k, :], ACT.Copy).then_inc(wh_done, 1)
            for k in range(1, KH):
                weight_sum_up(k)
            rounded_chunk(0, 1)
            act.wait_ge(b_ps, 1)
            act.wait_ge(rows_done, 5)
            act.activation(b_full[:], bank_b[0:ZS, :], ACT.Copy, scale=two_row[0:ZS, :]).then_inc(b_full_done, 1)
            act.wait_ge(conv_ps, 1)
            act.activation(yexp[:], bank_conv, ACT.Exp, scale=-1.0).then_inc(yexp_done, 1)
            act.wait_ge(sel_read, 3)
            act.activation(log_prior[:], lg[:, 0, :], ACT.Ln, bias=eps12[:, 0:1]).then_inc(lp_done, 1)
            rounded_chunk(1, 0)
            act.wait_ge(iota_done, 3)
            act.activation(table_use[:], part[:], ACT.Silu, scale=0.0)
            rounded_chunk(1, 2)
            def x_evacuate(b):
                act.wait_ge(xt_ps, b + 1)
                if b >= 2:
                    act.wait_ge(gu_ps, NC * (b - 1))
                act.activation(xq_t[:, b % 2, :, :], bank_xT[:, 0:H].rearrange("p (k e) -> p k e", k=KH),
                               ACT.Copy).then_inc(xt_done, 1)

            act.wait_ge(fold_ps, KH)
            for k in range(KH):
                act.activation(m_full[:, k, :], bank_m[k][:], ACT.Copy).then_inc(m_out, 1)
                if k == 1:
                    x_evacuate(0)
            act.wait_ge(mst_ps, 1)
            act.activation(ms_t, bank_ms[0:2 * ZL, :], ACT.Copy).then_inc(mst_done, 1)

            def weight_sum_down(i):
                j0, n, rows = DOWN_PARTS[i]
                act.wait_ge(ld_down[i], 16)
                weight_sum(2, i, raw_down[0:rows, j0:j0 + n, :], rows)

            def rounded_down(i):
                j0, n, rows = DOWN_PARTS[i]
                act.wait_ge(winv_done, 3)
                act.wait_ge(tern_out, 2 * NC + max(i - 1, 0))
                act.activation(tern_i[0:rows, i % 2, 0:n * H].rearrange("p (k f) -> p k f", k=n),
                               raw_down[0:rows, j0:j0 + n, :], ACT.Copy,
                               scale=winv[0:rows, 2:3]).then_inc(tern_int, 1)

            def silu_chunk(b, c):
                n = chunk_no(b, c)
                w = CHUNKS[c][1]
                act.wait_ge(gu_ps, n + 1)
                if n >= 2:
                    act.wait_ge(hmul_done, n - 1)
                act.activation(silu[:, n % 2, 0:w], bank_g[n % 2][:, 0:w], ACT.Silu,
                               scale=s_g[:, b:b + 1]).then_inc(silu_done, 1)

            def hidden_round(b):
                act.wait_ge(hscale_done, b + 1)
                if b >= 2:
                    act.wait_ge(hb_done, b - 1)
                act.activation(h_i[:, b % 2, :], hbuf[b % 2], ACT.Copy,
                               scale=hq[:, b:b + 1]).then_inc(hint_done, 1)

            def hidden_evacuate(b):
                for half, (j0, j1) in enumerate(((0, 6), (6, KF - 1))):
                    act.wait_ge(ht_ps, 2 * b + half + 1)
                    if b >= 2 and half == 0:
                        act.wait_ge(down_ps, b - 1)
                    src = bank_hT[half]
                    if half == 1:
                        act.activation(h_t[0:FL, b % 2, KF - 1, :], src[0:FL, (j1 - j0) * P:(j1 - j0 + 1) * P],
                                       ACT.Copy).then_inc(ht_done, 1)
                    act.activation(h_t[:, b % 2, j0:j1, :],
                                   src[:, 0:(j1 - j0) * P].rearrange("p (j e) -> p j e", e=P),
                                   ACT.Copy).then_inc(ht_done, 1)

            def m_high(k):
                act.wait_ge(m_out, k + 1)
                act.activation(m_h[:, k, :], m_full[:, k, :], ACT.Copy).then_inc(mh_done, 1)

            def x1_high(b):
                act.wait_ge(x1t_ps, b + 1)
                act.activation(x1t_h[:, b, :, :], bank_down[:].rearrange("p (k e) -> p k e", k=KH),
                               ACT.Copy).then_inc(x1h_done, 1)

            weight_sum_down(0)
            for b in range(NB + 2):
                if b < NB:
                    silu_chunk(b, 0)
                if b >= 3:
                    x1_high(b - 2)
                if b == 0:
                    weight_sum_down(1)
                    act.wait_ge(folds_ps, 1)
                    act.activation(ms_h, bank_ms[:, 0:KH * ZL].rearrange("p (k c) -> p k c", k=KH),
                                   ACT.Copy).then_inc(msh_done, 1)
                if b == 1:
                    rounded_down(0)
                if b < NB:
                    silu_chunk(b, 1)
                if 1 <= b <= NB:
                    hidden_evacuate(b - 1)
                if b + 1 < NB:
                    x_evacuate(b + 1)
                if b == 1:
                    rounded_down(2)
                if b == 2:
                    x1_high(0)
                if b < NB:
                    silu_chunk(b, 2)
                if b == 0:
                    weight_sum_down(2)
                    weight_sum_down(3)
                    weight_sum_down(4)
                if b == 1:
                    rounded_down(3)
                    rounded_down(4)
                if b < NB:
                    hidden_round(b)
                if b in (4, 5):
                    m_high(2 * (b - 4))
                    m_high(2 * (b - 4) + 1)
            for half in range(2):
                act.wait_ge(zlt_ps, half + 1)
                act.activation(zlt[:, 4 * half * P:4 * (half + 1) * P], bank_zt[half][0:2 * ZL, :],
                               ACT.Copy).then_inc(zlt_done, 1)
            act.wait_ge(lmax_done, 1)
            act.activation(ex[:], lg[:], ACT.Exp).then_inc(ex_done, 1)
            for i in range(2):
                act.wait_ge(zt_ps, i + 1)
                act.activation(zt[:, 4 * i:4 * i + 4, :], bank_zs[i][0:ZS, :].rearrange("p (b e) -> p b e", b=4),
                               ACT.Copy).then_inc(zt_done, 1)

        @block.tensor
        def _(pe):
            def keep_clock(n):
                for i in range(n):
                    pe.matmul(bank_warm[:], ident[:], t_iota[:], start=True, stop=True)

            pe.wait_ge(ident_done, 2)
            pe.wait_ge(iota_done, 6)
            keep_clock(WARM_UP)
            pe.wait_ge(lora_scaled, 1)
            for k in range(KH):
                pe.matmul(bank_delta[k][:], lora_bt[:, k * P:(k + 1) * P], lora_a,
                          start=True, stop=True).then_inc(delta_ps, 1)
            keep_clock(WARM_UP)

            def weight_total(i, dst, parts):
                pe.wait_ge(wsum_done[i], parts)
                pe.matmul(dst, ones[:], wsum[:, i, 0:parts], start=True, stop=True).then_inc(wtot_ps, 1)

            def selection(k):
                if k == 0:
                    pe.wait_ge(sel_done, 2)
                    pe.wait_ge(ld_exp, 48)
                if k < KH:
                    pe.matmul(bank_sel[:, k * ZL:k * ZL + ZC], l1a[:, k * P:(k + 1) * P], sel_er[:, 0:ZC],
                              start=True, stop=True)
                    pe.matmul(bank_sel[:, k * ZL + ZC:(k + 1) * ZL], rw[:, k * P:(k + 1) * P], sel_e[:],
                              start=True, stop=True)
                else:
                    for i in range(2):
                        mm = pe.matmul(bank_sel[:, KH * ZL + i * NACT:KH * ZL + (i + 1) * NACT], pr_bc[:, i, :],
                                       sel_e[:], start=True, stop=True)
                    mm.then_inc(sel_ps, 1)

            pe.wait_ge(delta_done, KH)
            def codebook(t, k):
                pe.matmul(bank_cb[k][:], diag_h[:, t, :], mask[t % 4][:, k, :], start=(t == 0), stop=False)
                return pe.matmul(bank_cb[k][:], diag_l[:, t, :], mask[t % 4][:, k, :], start=False,
                                 stop=(t == NT - 1))

            for t in range(4):
                pe.wait_ge(diag_done, 2 * (t + 1))
                pe.wait_ge(mask_done, t + 1)
                for k in range(KH):
                    mm = codebook(t, k)
                mm.then_inc(mask_used, 1)
                if t >= 1:
                    selection(t - 1)
            pe.wait_ge(diag_done, 2 * NT)
            for k in range(KH):
                for t in range(4, NT):
                    pe.wait_ge(mask_done, t + 1)
                    mm = codebook(t, k)
                mm.then_inc(cb_ps, 1)
            selection(KH - 1)
            selection(KH)
            pe.wait_ge(iota_done, 9)
            pe.wait_ge(delta_done, 2)
            pe.matmul(bank_b[0:ZS, :], sel_er[:], l1b, start=True, stop=False)
            pe.matmul(bank_b[0:ZS, :], bias_rows[:], bb[:], start=False, stop=True).then_inc(b_ps, 1)

            def x_transposes(b):
                pe.wait_ge(xq_done, b + 1)
                pe.wait_ge(ident_done, 2)
                if b == 0:
                    pe.wait_ge(wtot_read, 1)
                else:
                    pe.wait_ge(xt_done, b)
                for k in range(KH):
                    mm = pe.transpose(bank_xT[:, k * P:(k + 1) * P], xq_b[:, b % 2, k * P:(k + 1) * P],
                                      ident_b[:])
                mm.then_inc(xt_ps, 1)

            weight_total(0, bank_total[0], KH)
            pe.wait_ge(value_done, KH)
            pe.wait_ge(ch_done, 1)
            pe.wait_ge(cl_done, 1)

            def fold(k):
                n = 0
                for w, c in ((w_h, m_h), (w_h, m_l), (w_l, m_h)):
                    for i, o in enumerate(ROW_BLOCKS):
                        if k == 0 and w is w_h:
                            pe.wait_ge(wh_done, i + 1)
                        elif k == 0:
                            pe.wait_ge((wl_even, wl_odd)[o % 2], o // 2 + 1)
                        mm = pe.matmul(bank_m[k][:], w[:, o, k * P:(k + 1) * P], c[:, o, :],
                                       start=(n == 0), stop=(n == 3 * KH - 1))
                        n += 1
                mm.then_inc(fold_ps, 1)

            for k in range(KH):
                if k == 1:
                    pe.wait_ge(band_done, 1)
                    pe.wait_ge(ymean_done, 1)
                    pe.matmul(bank_conv, band[:], ymean[:], start=True, stop=True).then_inc(conv_ps, 1)
                if k == 2:
                    pe.wait_ge(sel_read, 3)
                if k == 3:
                    pe.wait_ge(b_full_done, 1)
                fold(k)
                if k == 1:
                    weight_total(1, bank_total[1], KH)

            def last_columns(dst, high, low):
                for k in range(KH):
                    if k < KH - 1:
                        pe.matmul(dst[0:2 * ZL, :], m_s[:, k, :], high(k), start=(k == 0), stop=False)
                    pe.matmul(dst[0:ZL, :], m_s[:, k, 0:ZL], low(k), start=False, stop=False)
                return pe.matmul(dst[0:2 * ZL, :], m_s[:, KH - 1, :], high(KH - 1), start=False, stop=True)

            pe.wait_ge(yexp_done, 1)
            last_columns(bank_ms, lambda o: w_h[:, o, :], lambda o: w_l[:, o, :]).then_inc(mst_ps, 1)

            x_transposes(0)

            def fold_last_columns():
                pe.wait_ge(mst_done, 1)
                pe.wait_ge(rows_done, 8)
                for k in range(KH):
                    mm = pe.matmul(bank_ms[:, k * ZL:(k + 1) * ZL], ms_t[:, k * P:(k + 1) * P],
                                   fold_two[0:2 * ZL, :], start=True, stop=True)
                mm.then_inc(folds_ps, 1)


            def gate_up(b, c):
                n = chunk_no(b, c)
                f0, w = CHUNKS[c]
                if c == 0:
                    pe.wait_ge(xt_done, b + 1)
                if b == 0:
                    pe.wait_ge(tern_out, NC + c + 1)
                if n == 0:
                    pe.wait_ge(wtot_read, 2)
                if n == 1:
                    pe.wait_ge(m_out, 2)
                if n >= 2:
                    pe.wait_ge(silu_done, n - 1)
                    pe.wait_ge(hmul_done, n - 1)
                for dst, w_t in ((bank_g[n % 2], tern_g), (bank_u[n % 2], tern_u)):
                    for k in range(KH):
                        mm = pe.matmul(dst[:, 0:w], xq_t[:, b % 2, k, :], w_t[:, k, f0:f0 + w],
                                       start=(k == 0), stop=(k == KH - 1))
                mm.then_inc(gu_ps, 1)

            def hidden_transposes(b):
                pe.wait_ge(hb_done, b + 1)
                for half, (j0, j1) in enumerate(((0, 6), (6, KF))):
                    if b == 0:
                        pe.wait_ge(m_out, KH)
                        pe.wait_ge(wtot_read, 3)
                    else:
                        pe.wait_ge(ht_done, 3 * (b - 1) + 1 + 2 * half)
                    for j in range(j0, j1):
                        rows = P if j < KF - 1 else FL
                        mm = pe.transpose(bank_hT[half][0:rows, (j - j0) * P:(j - j0 + 1) * P],
                                          h_b[:, b % 2, j * P:j * P + rows], ident_b[:])
                    mm.then_inc(ht_ps, 1)

            def down(b):
                if b == 0:
                    pe.wait_ge(msl_done, 1)
                else:
                    pe.wait_ge(x1l_done, b)
                pe.wait_ge(ht_done, 3 * (b + 1))
                firsts = [part[0] for part in DOWN_PARTS]
                for j in range(KF):
                    rows = P if j < KF - 1 else FL
                    if b == 0 and j in firsts:
                        pe.wait_ge(tern_out, 2 * NC + firsts.index(j) + 1)
                    mm = pe.matmul(bank_down[:], h_t[0:rows, b % 2, j, :], tern_d[0:rows, j, :],
                                   start=(j == 0), stop=(j == KF - 1))
                mm.then_inc(down_ps, 1)

            def x1_transposes(b):
                pe.wait_ge(x1_done, b + 1)
                for k in range(KH):
                    mm = pe.transpose(bank_down[:, k * P:(k + 1) * P], xs[:, b, k * P:(k + 1) * P], ident[:])
                mm.then_inc(x1t_ps, 1)

            def z_logits(half):
                b0 = 4 * half
                pe.wait_ge(x1l_done, b0 + 4)
                if half == 0:
                    pe.wait_ge(xt_done, NB)
                else:
                    pe.wait_ge(ht_done, 3 * NB)
                last_columns(bank_zt[half], lambda k: x1t_h[:, b0:b0 + 4, k, :],
                             lambda k: x1t_l[:, b0:b0 + 4, k, :]).then_inc(zlt_ps, 1)

            def z_rows():
                pe.wait_ge(zlt_done, 2)
                for b in range(NB):
                    mm = pe.matmul(bank_zr[:, b * ZL:(b + 1) * ZL], zlt[:, b * P:(b + 1) * P],
                                   fold_two[0:2 * ZL, :], start=True, stop=True)
                mm.then_inc(zl_ps, 1)

            def layer1(n_res):
                b, h0, h1 = RESULTS[n_res]
                if b < 4:
                    n = chunk_no(NB - 1, NC - 1) - (1 if b // 2 != (NC * NB - 1) % 2 else 0)
                    pe.wait_ge(silu_done, n + 1)
                    pe.wait_ge(hmul_done, n + 1)
                elif b == 4:
                    pe.wait_ge(x1l_done, NB)
                elif b == 5:
                    pe.wait_ge(ht_done, 3 * NB)
                else:
                    pe.wait_ge(res_done, n_res - 5)
                pe.wait_ge(x1l_done, b + 1)
                if b == 0:
                    pe.wait_ge(ml_done, KH)
                n = 0
                for k in range(KH):
                    for a, m in ((x1t_h, m_h), (x1t_h, m_l), (x1t_l, m_h)):
                        pe.matmul(bank_y[n_res][:, h0:h1], a[:, b, k, :], m[:, k, h0:h1], start=(n == 0), stop=False)
                        n += 1

            def experts(n_res):
                b, h0, h1 = RESULTS[n_res]
                pe.wait_ge(zt_done, b // 4 + 1)
                pe.wait_ge(b_done, 1)
                pe.matmul(bank_y[n_res][:, h0:h1], zt[:, b, :], b_stack[:, h0:h1], start=False,
                          stop=True).then_inc(y_ps, 1)

            for b in range(NB):
                gate_up(b, 0)
                if b == 0:
                    fold_last_columns()
                if b >= 3:
                    x1_transposes(b - 2)
                gate_up(b, 1)
                if b == 1:
                    pe.wait_ge(m_out, KH)
                    weight_total(2, bank_total[2], len(DOWN_PARTS))
                if b == 2:
                    down(0)
                if b >= 1:
                    hidden_transposes(b - 1)
                if b + 1 < NB:
                    x_transposes(b + 1)
                if b == 2:
                    x1_transposes(0)
                gate_up(b, 2)
                if b >= 2:
                    down(b - 1)
            last = NB - 1
            layer1(0)
            x1_transposes(last - 1)
            hidden_transposes(last)
            layer1(1)
            down(last)
            layer1(2)
            x1_transposes(last)
            z_logits(0)
            z_logits(1)
            layer1(3)
            z_rows()
            layer1(4)
            layer1(5)
            pe.wait_ge(zs_done, 1)
            for b in range(NB):
                mm = pe.transpose(bank_zs[b // 4][0:ZS, (b % 4) * P:(b % 4 + 1) * P], zstack[:, b, :], ident[:])
                if b % 4 == 3:
                    mm.then_inc(zt_ps, 1)
            for n in range(len(RESULTS)):
                if n >= 6:
                    layer1(n)
                experts(n)

        @block.vector
        def _(dve):
            links = [0]

            def link(ins):
                links[0] += 1
                ins.then_inc(dve_chain, 1)
                dve.wait_ge(dve_chain, links[0])

            dve.memset(wsum[:], 0.0).then_inc(eps_done, 1)
            link(dve.memset(eps12[:], 1e-12))
            dve.wait_ge(iota_done, 1)
            dve.tensor_scalar(ident[:], diff[:], 0.0, None, ALU.is_equal).then_inc(ident_done, 1)
            dve.tensor_scalar(ident_b[:], diff[:], 0.0, None, ALU.is_equal).then_inc(ident_done, 1)

            dve.wait_ge(ld_small, 16)
            link(dve.tensor_reduce(cbm[:, 0:1], cb, AX.X, ALU.max, apply_absolute_value=True))
            link(dve.tensor_scalar(cbm[:, 1:2], cbm[:, 0:1], 1e-8, None, ALU.max))
            link(dve.reciprocal(cbm[:, 2:3], cbm[:, 1:2]))
            link(dve.tensor_scalar(cbn[:], cb, cbm[:, 2:3], None, ALU.mult))
            link(dve.tensor_tensor(th[:], cbn[:, 0:NT], cbn[:, 1:NCB], ALU.add))
            dve.tensor_tensor(step[:], cbn[:, 1:NCB], cbn[:, 0:NT], ALU.subtract)
            link(dve.tensor_scalar(th[:], th[:], 0.5, None, ALU.mult))

            def t(i):
                return th[:, i:i + 1]
            link(dve.tensor_copy(step_h[:], step[:]))
            dve.tensor_tensor(step_l[:], step[:], step_h[:].bitcast(F32), ALU.subtract).then_inc(step_done, 1)
            dve.tensor_tensor(t(1), t(1), t(3), ALU.min)
            link(dve.tensor_tensor(t(5), t(5), t(3), ALU.max))
            dve.tensor_tensor(t(0), t(0), t(1), ALU.min)
            dve.tensor_tensor(t(6), t(6), t(5), ALU.max)
            dve.tensor_scalar(t(2), t(2), t(1), t(3), ALU.max, ALU.min)
            link(dve.tensor_scalar(t(4), t(4), t(3), t(5), ALU.max, ALU.min))
            link(dve.tensor_copy(act_f[:], act_i))
            dve.tensor_scalar(act_n[:], act_f[:], 0.0, float(NE), ALU.is_lt, ALU.mult)
            link(dve.tensor_copy(len_f[:], len_i))
            link(dve.tensor_tensor(act_f[:], act_f[:], act_n[:], ALU.add))
            link(dve.tensor_scalar(act_f[:], act_f[:], 0.0, float(NE - 1), ALU.max, ALU.min))
            dve.reciprocal(len_r[:], len_f[:])
            link(dve.tensor_scalar(act8[:], act_f[:], float(RK), None, ALU.mult))
            dve.wait_ge(iota_done, 4)
            act8_rep = act8[:].unsqueeze(2).broadcast_to([P, NACT, RK])
            for i in range(3):
                dve.tensor_tensor(sel_er[:, i * ZC:(i + 1) * ZC].rearrange("p (a r) -> p a r", a=NACT),
                                  pick[:], act8_rep, ALU.is_equal)
            dve.tensor_tensor(sel_e[:], part[0:NE, 0:1].broadcast_to([NE, NACT]), act_f[0:NE, :],
                              ALU.is_equal).then_inc(sel_done, 1)

            dve.wait_ge(scl_done, 1)
            link(dve.reciprocal(scl_inv[:], scl[:]))
            for k in range(KH):
                dve.wait_ge(delta_ps, k + 1)
                dve.wait_ge(ld_cond[k], 16)
                dve.tensor_tensor(cond[:, k, :], bank_delta[k][:], cond[:, k, :], ALU.add).then_inc(norm_step, 1)
                if k % 2 == 1:
                    dve.wait_ge(norm_step, k + 1)
                    v = cond[:, k, :].rearrange("p (g i) -> p g i", g=KH)
                    dve.tensor_tensor(v, v, scl_inv[:, k, :].unsqueeze(2).broadcast_to([P, KH, GROUP]),
                                      ALU.mult).then_inc(norm_done, 1)
                if k == 1:
                    dve.wait_ge(ld_exp, 48)
                    dve.tensor_copy(pr_bc[:], pr.unsqueeze(2).broadcast_to([NE, 2, P])).then_inc(sel_done, 1)
            dve.wait_ge(norm_done, KH)

            def x_sum(b):
                dve.wait_ge(ld_x[b], 16)
                link(dve.scalar_tensor_tensor(junk[:], t_iota[:], len_f[:, b:b + 1], xs[:, b, :], ALU.is_lt,
                                              ALU.mult, accum_out=ysum[:, b:b + 1]))

            for i in range(NT):
                if i >= 4:
                    dve.wait_ge(mask_used, i - 3)
                dve.tensor_scalar(mask[i % 4], cond[:], t(i), None, ALU.is_gt).then_inc(mask_done, 1)
                if i == 3:
                    x_sum(0)
                    x_sum(1)

            def weight_scale(i, src):
                dve.wait_ge(wtot_ps, i + 1)
                dve.tensor_reduce(wtot[:, i:i + 1], src, AX.X, ALU.add).then_inc(wtot_read, 1)
                dve.wait_ge(wtot_read, i + 1)
                link(dve.tensor_scalar(wscale[:, i:i + 1], wtot[:, i:i + 1], 1.0 / NW, EPS, ALU.mult, ALU.max))
                dve.tensor_scalar(w127[:, i:i + 1], wscale[:, i:i + 1], 1.0 / QMAX, None, ALU.mult)
                dve.reciprocal(winv[:, i:i + 1], wscale[:, i:i + 1]).then_inc(winv_done, 1)
                dve.wait_ge(winv_done, i + 1)

            def ternary(i, dst, src, n_before, rows=P, rounded_by_act=0):
                n = src.shape[1] * src.shape[2]
                tmp = tern_i[0:rows, n_before % 2, 0:n].rearrange("p (k f) -> p k f", k=src.shape[1])
                if rounded_by_act:
                    dve.wait_ge(tern_int, rounded_by_act)
                else:
                    if n_before >= 1:
                        dve.wait_ge(tern_out, n_before)
                    link(dve.tensor_scalar(tmp, src, winv[0:rows, i:i + 1], None, ALU.mult))
                dve.tensor_scalar(dst, tmp, 1.0, -1.0, ALU.min, ALU.max).then_inc(tern_out, 1)

            def x_max(b0, b1):
                link(dve.tensor_reduce(rmax[:, b0:b1], xs[:, b0:b1, :], AX.X, ALU.max, apply_absolute_value=True))

            def ternary_chunk(i, c, rounded_by_act=0):
                f0, w = CHUNKS[c]
                ternary(i, (tern_g, tern_u)[i][:, :, f0:f0 + w], (raw_gate, raw_up)[i][:, :, f0:f0 + w],
                        i * NC + c, rounded_by_act=rounded_by_act)

            for k in range(KH):
                x_sum(2 + k)
                dve.wait_ge(cb_ps, k + 1)
                v = cond[:, k, :].rearrange("p (g i) -> p g i", g=KH)
                dve.scalar_tensor_tensor(v, bank_cb[k][:].rearrange("p (g i) -> p g i", g=KH), cbn[:, 0:1],
                                         scl[:, k, :].unsqueeze(2).broadcast_to([P, KH, GROUP]),
                                         ALU.add, ALU.mult).then_inc(value_done, 1)
            dve.wait_ge(delta_done, KH)
            dve.wait_ge(value_done, KH)
            for k in range(1, KH, 2):
                dve.tensor_tensor(cond[:, k, :], cond[:, k, :], delta[:, k, :], ALU.add).then_inc(weff_odd, 1)
            for i, k in enumerate(ROW_BLOCKS):
                if k % 2 == 1:
                    dve.wait_ge(wh_done, i + 1)
                    dve.tensor_tensor(w_l[:, k, :], cond[:, k, :], w_h[:, k, :].bitcast(F32),
                                      ALU.subtract).then_inc(wl_odd, 1)
            x_sum(6)
            x_sum(7)
            dve.tensor_tensor(ymean[:], ysum[:], len_r[:], ALU.mult).then_inc(ymean_done, 1)
            weight_scale(0, bank_total[0])
            ternary_chunk(0, 0)
            dve.wait_ge(sel_ps, 1)
            sel_v = bank_sel[:, 0:KH * ZL].rearrange("p (k c) -> p k c", k=KH)
            dve.tensor_copy(ms_h, sel_v).then_inc(sel_read, 1)
            dve.wait_ge(sel_read, 1)
            dve.tensor_tensor(ms_l, sel_v, ms_h.bitcast(F32), ALU.subtract).then_inc(sel_read, 1)
            dve.tensor_copy(lg[:, 0:2, :], bank_sel[:, KH * ZL:KH * ZL + 2 * NACT]
                            .rearrange("p (i a) -> p i a", i=2)).then_inc(sel_read, 1)
            ternary_chunk(0, 1, rounded_by_act=1)
            weight_scale(1, bank_total[1])
            ternary_chunk(0, 2)
            x_max(0, 2)
            ternary_chunk(1, 0, rounded_by_act=2)

            def x_scales(b0, b1):
                o = slice(b0, b1)
                link(dve.tensor_tensor(arow[:, o], rmax[:, o], gate[:, o], ALU.mult))
                link(dve.tensor_scalar(arow[:, o], arow[:, o], EPS, None, ALU.max))
                link(dve.reciprocal(qx[:, o], arow[:, o]))
                dve.tensor_scalar(s_g[:, o], arow[:, o], w127[:, 0:1], None, ALU.mult)
                dve.tensor_scalar(s_u[:, o], arow[:, o], w127[:, 1:2], None, ALU.mult)
                dve.tensor_scalar(qx[:, o], qx[:, o], QMAX, None, ALU.mult).then_inc(qx_done, 1)
                dve.wait_ge(qx_done, 1 + b0 // 2)

            dve.wait_ge(yexp_done, 1)
            link(dve.tensor_scalar(yexp[:], yexp[:], 1.0, None, ALU.add))
            link(dve.reciprocal(gate[:], yexp[:]))
            x_scales(0, 2)

            def x_quantise(b):
                link(dve.tensor_scalar(xq_i[:, b % 2, :], xs[:, b, :], gate[:, b:b + 1], qx[:, b:b + 1],
                                       ALU.mult, ALU.mult))
                dve.tensor_copy(xq_b[:, b % 2, :], xq_i[:, b % 2, :]).then_inc(xq_done, 1)

            x_quantise(0)
            ternary_chunk(1, 1)
            ternary_chunk(1, 2, rounded_by_act=3)

            def stacked_b():
                dve.wait_ge(b_full_done, 1)
                dve.wait_ge(rows_done, 5)
                link(dve.tensor_copy(b_high, b_full[:]))
                link(dve.tensor_scalar(b_full[:], b_full[:], low_row[0:ZS, :], None, ALU.mult))
                dve.scalar_tensor_tensor(b_stack[:], b_high.bitcast(F32), sign_row[0:ZS, :], b_full[:],
                                         ALU.mult, ALU.add).then_inc(b_done, 1)
                dve.wait_ge(lp_done, 1)
                link(dve.tensor_tensor(log_prior[:], log_prior[:], lg[:, 1, :], ALU.add))

            x_max(2, 4)
            x_scales(2, 4)

            def ternary_down(i):
                j0, n, rows = DOWN_PARTS[i]
                ternary(2, tern_d[0:rows, j0:j0 + n, :], raw_down[0:rows, j0:j0 + n, :], 2 * NC + i,
                        rows, rounded_by_act=4 + DOWN_BY_ACT.index(i) if i in DOWN_BY_ACT else 0)

            def hidden_chunk(b, c):
                n = chunk_no(b, c)
                f0, w = CHUNKS[c]
                dve.wait_ge(silu_done, n + 1)
                if c == 0 and b >= 2:
                    dve.wait_ge(hint_done, b - 1)
                if n == 0:
                    dve.wait_ge(tern_out, 2 * NC)
                hs = hbuf[b % 2][:, f0:f0 + w]
                dve.tensor_tensor(hs, bank_u[n % 2][:, 0:w], silu[:, n % 2, 0:w], ALU.mult)\
                    .then_inc(hmul_done, 1)
                dve.wait_ge(hmul_done, n + 1)
                link(dve.tensor_reduce(hmax[:, b % 2, c:c + 1], hs, AX.X, ALU.max, apply_absolute_value=True))

            def hidden_scale(b):
                o = slice(b, b + 1)
                link(dve.tensor_reduce(hred[:, o], hmax[:, b % 2, :], AX.X, ALU.max))
                link(dve.tensor_scalar(harow[:, o], hred[:, o], s_u[:, o], EPS, ALU.mult, ALU.max))
                link(dve.reciprocal(hrec[:, o], harow[:, o]))
                dve.tensor_scalar(hq[:, o], hrec[:, o], QMAX, s_u[:, o], ALU.mult, ALU.mult)\
                    .then_inc(hscale_done, 1)

            def hidden_bf16(b):
                dve.wait_ge(hint_done, b + 1)
                if b >= 2:
                    dve.wait_ge(ht_ps, 2 * (b - 1))
                dve.tensor_copy(h_b[:, b % 2, :], h_i[:, b % 2, :]).then_inc(hb_done, 1)

            def residual(b):
                o = slice(b, b + 1)
                link(dve.tensor_scalar(s_d[:, o], harow[:, o], w127[:, 2:3], None, ALU.mult))
                dve.wait_ge(down_ps, b + 1)
                dve.scalar_tensor_tensor(xs[:, b, :], bank_down[:], s_d[:, o], xs[:, b, :],
                                         ALU.mult, ALU.add).then_inc(x1_done, 1)

            def x1_low(b):
                dve.wait_ge(x1h_done, b + 1)
                dve.tensor_tensor(x1t_l[:, b, :, :], bank_down[:].rearrange("p (k e) -> p k e", k=KH),
                                  x1t_h[:, b, :, :].bitcast(F32), ALU.subtract).then_inc(x1l_done, 1)

            for b in range(NB + 2):
                if 1 <= b <= NB:
                    hidden_bf16(b - 1)
                if b == 2:
                    residual(0)
                if b < NB:
                    hidden_chunk(b, 0)
                if b == 0:
                    dve.wait_ge(msh_done, 1)
                    dve.tensor_tensor(ms_l, bank_ms[:, 0:KH * ZL].rearrange("p (k c) -> p k c", k=KH),
                                      ms_h.bitcast(F32), ALU.subtract).then_inc(msl_done, 1)
                if b == 1:
                    ternary_down(0)
                if b >= 3:
                    x1_low(b - 2)
                if b < NB:
                    hidden_chunk(b, 1)
                if b == 2:
                    x1_low(0)
                    x_scales(4, 6)
                if b == 1:
                    ternary_down(1)
                    ternary_down(2)
                if b < NB:
                    hidden_chunk(b, 2)
                    hidden_scale(b)
                if b == 0:
                    x_max(5, 6)
                    weight_scale(2, bank_total[2])
                if b == 1:
                    ternary_down(3)
                    ternary_down(4)
                    x_max(4, 5)
                if 2 <= b <= NB:
                    residual(b - 1)
                if b == 2:
                    x_max(6, NB)
                    x_scales(6, NB)
                if b == 5:
                    stacked_b()

            dve.wait_ge(ml_done, KH)
            dve.wait_ge(zl_ps, 1)
            link(dve.tensor_copy(zl[:], bank_zr[:, 0:NB * ZL].rearrange("p (b c) -> p b c", b=NB)))
            link(dve.tensor_tensor(lg[:], zl[:, :, ZC:ZL], log_prior[:].unsqueeze(1).broadcast_to([P, NB, NACT]),
                                   ALU.add))
            link(dve.tensor_reduce(lmax[:], lg[:], AX.X, ALU.max))
            dve.tensor_tensor(lg[:], lg[:], lmax[:].unsqueeze(2).broadcast_to([P, NB, NACT]),
                              ALU.subtract).then_inc(lmax_done, 1)
            dve.wait_ge(ex_done, 1)
            link(dve.tensor_reduce(esum[:], ex[:], AX.X, ALU.add))
            link(dve.reciprocal(esum[:], esum[:]))
            link(dve.tensor_tensor(alpha[:], ex[:], esum[:].unsqueeze(2).broadcast_to([P, NB, NACT]), ALU.mult))
            for a in range(NACT):
                ins = dve.tensor_tensor(zz[:, :, a * RK:(a + 1) * RK], zl[:, :, a * RK:(a + 1) * RK],
                                        alpha[:, :, a:a + 1].broadcast_to([P, NB, RK]), ALU.mult)
            link(ins)
            link(dve.tensor_copy(zz_h[:], zz[:]))
            dve.memset(zstack[:, :, 3 * ZC:ZS], 1.0)
            high = zz_h[:].bitcast(F32)
            dve.tensor_copy(zstack[:, :, 0:ZC], high)
            dve.tensor_copy(zstack[:, :, 2 * ZC:3 * ZC], high)
            dve.tensor_tensor(zstack[:, :, ZC:2 * ZC], zz[:], high, ALU.subtract).then_inc(zs_done, 1)
            for n, (b, h0, h1) in enumerate(RESULTS):
                dve.wait_ge(y_ps, n + 1)
                dve.tensor_tensor(xs[:, b, h0:h1], bank_y[n][:, h0:h1], xs[:, b, h0:h1],
                                  ALU.add).then_inc(res_done, 1)


def kernel(x, itok_B_9_3973, condB_codebook, L0_cond_conv_w, L0_ffn_w_gate, L0_ffn_w_up, L0_ffn_w_down,
           L1_cond_weight, L1_cond_scale_log, L1_cond_lora_A, L1_cond_lora_B, L1_ffn_W_base, L1_ffn_b_base,
           L1_ffn_lora_A, L1_ffn_lora_B, L1_ffn_router_W, L1_ffn_router_b, L1_ffn_domain_prior, L1_ffn_active):
    import numpy as np
    import concourse.bacc as bacc
    from concourse.bass_utils import run_bass_kernel_spmd

    n = np.asarray
    layout = {
        "x": n(x),
        "small": np.concatenate([n(condB_codebook), n(L0_cond_conv_w).reshape(TAPS),
                                 n(itok_B_9_3973).view(np.float32), n(L1_ffn_active).view(np.float32)]),
        "w_gate_t": n(L0_ffn_w_gate).T,
        "w_up_t": n(L0_ffn_w_up).T,
        "w_down_t": n(L0_ffn_w_down).T,
        "cond_w": n(L1_cond_weight),
        "scale_log": n(L1_cond_scale_log).reshape(KH, P, KH).transpose(1, 0, 2),
        "lora0": np.stack([n(L1_cond_lora_A), n(L1_cond_lora_B).T], axis=1),
        "w_base_t": n(L1_ffn_W_base).T,
        "b_base": n(L1_ffn_b_base).reshape(1, H),
        "lora1": np.stack([n(L1_ffn_lora_A).reshape(NE * RK, H),
                           n(L1_ffn_lora_B).transpose(0, 2, 1).reshape(NE * RK, H)], axis=1),
        "router": np.concatenate([n(L1_ffn_router_W), n(L1_ffn_domain_prior).reshape(NE, 1),
                                  n(L1_ffn_router_b).reshape(NE, 1)], axis=1),
    }
    nc = bacc.Bacc("TRN2", target_bir_lowering=False, num_devices=1)
    arrays, args = {}, {}
    for name, a in layout.items():
        a = np.ascontiguousarray(a)
        arrays[f"in_{name}"] = a
        args[name] = nc.dram_tensor(f"in_{name}", a.shape, mybir.dt.from_np(a.dtype), kind="ExternalInput").ap()
    args["out"] = nc.dram_tensor("out_x", (NB, E, H), F32, kind="ExternalOutput").ap()
    build(nc, **args)
    r = run_bass_kernel_spmd(nc, [arrays], core_ids=[0])
    return r.results[0]["out_x"]
```
